# Optimizing a Trainium2 kernel written in Bass

```python
import numpy as np
import jax
import jax.numpy as jnp

def _softmax(x, axis=-1):
    return jax.nn.softmax(x, axis=axis)

def _gelu(x):
    return jax.nn.gelu(x, approximate=True)

def _silu(x):
    return jax.nn.silu(x)

def _sigmoid(x):
    return jax.nn.sigmoid(x)

def _layernorm(x, axis=-1, eps=1e-05):
    m = jnp.mean(x, axis=axis, keepdims=True)
    v = jnp.var(x, axis=axis, keepdims=True)
    return (x - m) / jnp.sqrt(v + eps)

def _scatter_add(tgt, idx, src, axis=0):
    return tgt.at[idx].add(src)

def _segment_sum(src, seg, n):
    return jax.ops.segment_sum(src, seg, n)
kernel_name = 'mk_gnn_ffn_d1_gnn_r8_68f33d'

def setup_inputs(seed: int=0):
    np.random.seed(seed)
    _w = jnp.asarray

    def _rec_inputs():
        import jax
        import jax.numpy as jnp
        _gk = jax.random.key(seed)
        x = -0.0003713 + 1 * jax.random.normal(jax.random.fold_in(_gk, 1), (6250, 256), jnp.float32)
        _s = jax.random.randint(jax.random.fold_in(_gk, 2), (50000,), 0, 6250, jnp.int32)
        _d = jax.random.randint(jax.random.fold_in(_gk, 3), (50000,), 0, 6250, jnp.int32)
        _loop = jnp.arange(6250, dtype=jnp.int32)
        src = jnp.concatenate([_s, _d, _loop])
        dst = jnp.concatenate([_d, _s, _loop])
        _o = jnp.argsort(dst, stable=True)
        src = src[_o]
        dst = dst[_o]
        edge_weight = jax.random.uniform(jax.random.fold_in(_gk, 12), (106250,), jnp.float32, 0.0, 0.999998)
        return (x, src, dst, edge_weight)
    x, src, dst, edge_weight = _rec_inputs()

    def _L0_gnn_setup():
        import jax, jax.numpy as jnp
        import numpy as np
        N = 6250
        E = 100000
        F_IN = 256
        F_OUT = 256
        key = jax.random.key(seed)
        k1, k2, k3, k4, k5, k6 = jax.random.split(key, 6)
        x = jax.random.normal(k1, (N, F_IN), dtype=jnp.float32)
        edge_index = jax.random.randint(k2, (2, E), 0, N, dtype=jnp.int64)
        edge_values = jax.random.uniform(k3, (E,), dtype=jnp.float32)
        s_w = float(np.sqrt(6.0 / (F_IN + F_OUT)))
        s_a = float(np.sqrt(6.0 / (F_OUT + 1)))
        W = jax.random.uniform(k4, (F_IN, F_OUT), dtype=jnp.float32, minval=-s_w, maxval=s_w)
        a1 = jax.random.uniform(k5, (F_OUT, 1), dtype=jnp.float32, minval=-s_a, maxval=s_a)
        a2 = jax.random.uniform(k6, (F_OUT, 1), dtype=jnp.float32, minval=-s_a, maxval=s_a)
        return {'x': x, 'edge_index': edge_index, 'edge_values': edge_values, 'W': W, 'a1': a1, 'a2': a2}
    _L0_gnn_all = _L0_gnn_setup()
    _L0_gnn_in = {k: v for k, v in _L0_gnn_all.items() if k in ('W', 'a1', 'a2')}
    del _L0_gnn_all

    def _L0_ffn_setup():
        import jax, jax.numpy as jnp
        import numpy as np
        DIM = 256
        H = 8
        D = 64
        G = 64
        INNER = H * D
        SCALE = D ** (-0.5)
        key = jax.random.key(seed)
        ks = jax.random.split(key, 12)
        B, N = (4, 2048)
        x = jax.random.normal(ks[0], (B, N, DIM), dtype=jnp.float32)
        s = lambda fan_in: 1.0 / np.sqrt(fan_in)
        W_fx = jax.random.normal(ks[1], (DIM, INNER), dtype=jnp.float32) * s(DIM)
        b_fx = jnp.zeros((INNER,), dtype=jnp.float32)
        W_x = jax.random.normal(ks[2], (DIM, INNER), dtype=jnp.float32) * s(DIM)
        b_x = jnp.zeros((INNER,), dtype=jnp.float32)
        A = jax.random.normal(ks[3], (G, D), dtype=jnp.float32)
        Q, _ = jnp.linalg.qr(A.T)
        W_slice = Q[:, :G].astype(jnp.float32)
        b_slice = jnp.zeros((G,), dtype=jnp.float32)
        W_q = jax.random.normal(ks[4], (D, D), dtype=jnp.float32) * s(D)
        W_k = jax.random.normal(ks[5], (D, D), dtype=jnp.float32) * s(D)
        W_v = jax.random.normal(ks[6], (D, D), dtype=jnp.float32) * s(D)
        W_out = jax.random.normal(ks[7], (INNER, DIM), dtype=jnp.float32) * s(INNER)
        b_out = jnp.zeros((DIM,), dtype=jnp.float32)
        temperature = jnp.ones((1, H, 1, 1), dtype=jnp.float32) * 0.5
        return {'x': x, 'W_fx': W_fx, 'b_fx': b_fx, 'W_x': W_x, 'b_x': b_x, 'W_slice': W_slice, 'b_slice': b_slice, 'W_q': W_q, 'W_k': W_k, 'W_v': W_v, 'W_out': W_out, 'b_out': b_out, 'temperature': temperature}
    _L0_ffn_all = _L0_ffn_setup()
    _L0_ffn_in = {k: v for k, v in _L0_ffn_all.items() if k in ('W_fx', 'b_fx', 'W_x', 'b_x', 'W_slice', 'b_slice', 'W_q', 'W_k', 'W_v', 'W_out', 'b_out', 'temperature')}
    del _L0_ffn_all
    return {'x': x, 'src': src, 'dst': dst, 'edge_weight': edge_weight, 'L0_gnn_W': _L0_gnn_in['W'], 'L0_gnn_a1': _L0_gnn_in['a1'], 'L0_gnn_a2': _L0_gnn_in['a2'], 'L0_ffn_W_fx': _L0_ffn_in['W_fx'], 'L0_ffn_b_fx': _L0_ffn_in['b_fx'], 'L0_ffn_W_x': _L0_ffn_in['W_x'], 'L0_ffn_b_x': _L0_ffn_in['b_x'], 'L0_ffn_W_slice': _L0_ffn_in['W_slice'], 'L0_ffn_b_slice': _L0_ffn_in['b_slice'], 'L0_ffn_W_q': _L0_ffn_in['W_q'], 'L0_ffn_W_k': _L0_ffn_in['W_k'], 'L0_ffn_W_v': _L0_ffn_in['W_v'], 'L0_ffn_W_out': _L0_ffn_in['W_out'], 'L0_ffn_b_out': _L0_ffn_in['b_out'], 'L0_ffn_temperature': _L0_ffn_in['temperature']}

def reference(x, src, dst, edge_weight, L0_gnn_W, L0_gnn_a1, L0_gnn_a2, L0_ffn_W_fx, L0_ffn_b_fx, L0_ffn_W_x, L0_ffn_b_x, L0_ffn_W_slice, L0_ffn_b_slice, L0_ffn_W_q, L0_ffn_W_k, L0_ffn_W_v, L0_ffn_W_out, L0_ffn_b_out, L0_ffn_temperature):
    import jax
    import jax.numpy as jnp

    def _L0_gnn_ref(x, edge_index, edge_values, W, a1, a2):
        import jax, jax.numpy as jnp
        import numpy as np
        N = 6250
        E = 100000
        F_IN = 256
        F_OUT = 256
        n = x.shape[0]
        row, col = (edge_index[0], edge_index[1])
        support = x @ W
        r_D = jax.nn.sigmoid(support @ a2)
        gated = r_D * support
        msg = gated[col] * edge_values[:, None]
        out = jax.ops.segment_sum(msg, row, num_segments=n)
        sumnorm = jax.ops.segment_sum(edge_values * r_D[col, 0], row, num_segments=n)
        out = out / sumnorm[:, None]
        l_D = jax.nn.softplus(out @ a1)
        out = jnp.maximum(out, 0.0) + l_D * jnp.minimum(out, 0.0)
        out = jax.nn.elu(out)
        return out

    def _L0_ffn_ref(x, W_fx, b_fx, W_x, b_x, W_slice, b_slice, W_q, W_k, W_v, W_out, b_out, temperature):
        import jax, jax.numpy as jnp
        import numpy as np
        DIM = 256
        H = 8
        D = 64
        G = 64
        INNER = H * D
        SCALE = D ** (-0.5)
        B, N, _ = x.shape
        fx_mid = (x @ W_fx + b_fx).reshape(B, N, H, D).transpose(0, 2, 1, 3)
        x_mid = (x @ W_x + b_x).reshape(B, N, H, D).transpose(0, 2, 1, 3)
        temp = jnp.clip(temperature, 0.1, 5.0)
        slice_weights = jax.nn.softmax((x_mid @ W_slice + b_slice) / temp, axis=-1)
        slice_norm = slice_weights.sum(axis=2)
        slice_token = jnp.einsum('bhnc,bhng->bhgc', fx_mid, slice_weights)
        slice_token = slice_token / (slice_norm[..., None] + 1e-05)
        q = slice_token @ W_q
        k = slice_token @ W_k
        v = slice_token @ W_v
        attn = jax.nn.softmax(jnp.einsum('bhgc,bhkc->bhgk', q, k) * SCALE, axis=-1)
        out_slice = jnp.einsum('bhgk,bhkc->bhgc', attn, v)
        out_x = jnp.einsum('bhgc,bhng->bhnc', out_slice, slice_weights)
        out_x = out_x.transpose(0, 2, 1, 3).reshape(B, N, INNER)
        return out_x @ W_out + b_out
    edge_index = jnp.stack([src, dst])
    x = x + _L0_gnn_ref(_layernorm(x, axis=-1), edge_index, edge_weight, L0_gnn_W, L0_gnn_a1, L0_gnn_a2)
    x = x + _L0_ffn_ref(_layernorm(x, axis=-1)[None], L0_ffn_W_fx, L0_ffn_b_fx, L0_ffn_W_x, L0_ffn_b_x, L0_ffn_W_slice, L0_ffn_b_slice, L0_ffn_W_q, L0_ffn_W_k, L0_ffn_W_v, L0_ffn_W_out, L0_ffn_b_out, L0_ffn_temperature)[0]
    return x

_drawn_inputs = setup_inputs


def setup_inputs(seed=0):
    import zlib

    import numpy as np

    out = dict(_drawn_inputs(seed))
    spreads = {'L0_ffn_b_fx': (0.0, 0.1),
     'L0_ffn_b_x': (0.0, 0.8),
     'L0_ffn_b_slice': (0.0, 2.0),
     'L0_ffn_b_out': (0.0, 0.1),
     'L0_ffn_temperature': (0.5, 0.6)}
    factors = {'L0_ffn_W_x': 8.0, 'L0_ffn_W_slice': 8.0, 'L0_ffn_W_q': 8.0, 'L0_ffn_W_k': 8.0}
    for name, (base, spread) in spreads.items():
        noise = np.random.default_rng([zlib.crc32(name.encode()), seed]).standard_normal(out[name].shape)
        drawn = base * np.exp(spread * noise) if base else spread * noise
        out[name] = jnp.asarray(drawn.astype(out[name].dtype))
    for name, factor in factors.items():
        out[name] = (out[name] * factor).astype(out[name].dtype)
    return out
```

```python
import numpy as np
from contextlib import ExitStack

import concourse.bass as bass
from concourse import mybir

F32 = mybir.dt.float32
BF16 = mybir.dt.bfloat16
I32 = mybir.dt.int32
U8 = mybir.dt.uint8
ALU = mybir.AluOpType
ACT = mybir.ActivationFunctionType
AX = mybir.AxisListType

P = 128
N = 6250
F = 256
E = 106250
NB = -(-N // P)
TAIL = N - (NB - 1) * P
ECOL = E // P
EREST = E - ECOL * P
EC = 832
CAP = -(-(E // P + NB) // 16) * 16
PITCH = CAP + EC - ECOL
H = 8
G = 64
D = 64
HG = H * G
NP2 = H // 2
GW = F + 1
U = 8
Q = 7
assert NB % Q == 0
EPS = 1e-5
SCALE = float(D) ** -0.5
SEGB = (0, 1, 2, 5)
ds = bass.ds


class Chain:

    def __init__(self, eng, sem):
        self.eng, self.sem, self.n, self.loop, self.per = eng, sem, 0, 0, 0

    def __call__(self, ins):
        ins.then_inc(self.sem, 1)
        self.n += 1
        self.eng.wait_ge(self.sem, self.loop + self.n)
        return self

    def enter(self, i, first, per):
        self.loop = (i - first) * per

    def leave(self, count, per):
        self.loop = 0
        self.n += (count - 1) * per


def build(nc, x, src, dst, ew, W, a1, a2, W_fx, b_fx, W_x, b_x, W_slice, b_slice, W_q, W_k, W_v,
          W_out, b_out, temp, out, gtab, srt):
    with ExitStack() as ctx:
        def sb(name, shape, dt=F32):
            return ctx.enter_context(nc.sbuf_tensor(name, shape, dt))

        def sem(name):
            return ctx.enter_context(nc.semaphore(name))

        bank = [ctx.enter_context(nc.psum_tensor(f"bank{i}", [P, 512], F32)) for i in range(8)]

        acc = sb("acc", [P, NB, GW])
        big = sb("big", [P, 4 * NB * P])
        xs = big[:, 0:NB * F].rearrange("p (b f) -> p b f", b=NB)
        swt = big[:, :].rearrange("p (c n) -> p c n", c=4)

        class Carve:

            def __init__(self):
                self.at = NB * F

            def __call__(self, n, dt=F32):
                v = big[:, self.at:self.at + n]
                self.at += n
                assert self.at <= 4 * NB * P
                return v if dt == F32 else v.bitcast(dt)

        carve = Carve()
        rowi = carve(EC, I32)
        coli = carve(EC, I32)
        ewi = carve(EC, I32)
        rec = carve(2 * EC, I32).rearrange("p (j k) -> p j k", k=2)
        hif = carve(EC)
        slotf = carve(EC)
        scan = carve(EC)
        sloti = carve(EC, I32)
        tmpi = carve(EC, I32)
        sf = carve(EC)
        zero_rec = carve(2 * PITCH, I32)
        mask = sb("mask", [P, EC], U8)
        onesb = sb("onesb", [P, EC], BF16)
        carve = Carve()
        srec = carve(2 * PITCH, I32).rearrange("p (t k) -> p t k", k=2)
        colx = carve(CAP, I32)
        lof = carve(CAP)
        offi = carve(CAP, I32)
        iota_t = carve(CAP)
        ge = carve(CAP)
        rows = carve(2 * U * GW).rearrange("p (u w) -> p u w", w=GW)
        S = carve(4 * P).rearrange("p (u r) -> p u r", r=P)
        sewf = srec.bitcast(F32)
        iota = sb("iota", [P, P])
        iotap = sb("iotap", [P, 1])
        ident = sb("ident", [P, P])
        lower = sb("lower", [P, P])
        ones = sb("ones", [P, P])
        valid = sb("valid", [P, NB])
        padf = sb("padf", [P, 1])
        Wg = sb("Wg", [P, 2, GW])
        a1b = sb("a1b", [P, F])
        a2b = sb("a2b", [P, F])
        Wxs = sb("Wxs", [P, 2, HG])
        bxs = sb("bxs", [1, HG])
        Wfx = sb("Wfx", [P, 2, HG])
        bfx = sb("bfx", [1, HG])
        zrow = sb("zrow", [1, HG])
        Wo = sb("Wo", [P, NP2, F])
        bob = sb("bob", [G, F])
        W2 = sb("W2", [P, 4, P])
        tb = sb("tb", [P, H])
        bsr = sb("bsr", [1, G])
        bxc = sb("bxc", [P, NP2])
        wide = acc[:, 0:8, :]
        Wxr = wide[:, 0:4, 0:F].rearrange("p (k m) f -> p k m f", k=2)
        WxT = wide[:, 4:8, 0:F]
        cnt = sb("cnt", [P, NB])
        nti = sb("nti", [P, NB], I32)
        ntf = sb("ntf", [P, NB])
        ctf = sb("ctf", [P, NB])
        base = sb("base", [P, NB])
        ctcol = sb("ctcol", [NB, 1])
        st6 = sb("st6", [P, NB, 6])
        part = sb("part", [P, Q])
        var = sb("var", [P, NB])
        mean = sb("mean", [P, NB])
        lnv = sb("lnv", [P, NB])
        rstd = sb("rstd", [P, NB])
        nmr = sb("nmr", [P, NB])
        nwt = sb("nwt", [P, NB])
        rinv = sb("rinv", [P, NB])
        zd = sb("zd", [P, NB])
        za = sb("za", [P, NB])
        ld = sb("ld", [P, NB])
        sm = sb("sm", [P, 2, 4])
        hm = sb("hm", [P, 2, 3, H])
        ring_i = sb("ring_i", [P, 2, U], I32)
        ring_r = sb("ring_r", [P, 2, U, 2], I32)
        xn = sb("xn", [P, 2, F])
        xT = sb("xT", [P, 2, F])
        Gt = sb("Gt", [P, 2, GW])
        pos = sb("pos", [P, 2, F])
        neg = sb("neg", [P, 2, F])
        lg = sb("lg", [P, 2, HG])
        sw = sb("sw", [P, 2, HG])
        Mn = lg[:, :, :].rearrange("p a b -> p (a b)").rearrange("p (c f) -> p c f", f=F)
        MnT = sw[:, :, :]
        nrm = sb("nrm", [P, 3, NP2])
        nbT = sb("nbT", [1, HG])
        def pairs(t, n=P):
            return t.rearrange("p (c n) -> p c n", n=n)

        def flat(t):
            return t.rearrange("p a b -> p (a b)")

        tokd = pairs(flat(neg[:, :, :]))
        qd = pairs(flat(xT[:, :, :]))
        vd = pairs(flat(xn[:, :, :]))
        aT = pairs(flat(pos[:, :, :]))
        oT = pairs(flat(Wg[:, :, :])[:, 0:HG])
        ad = pairs(Wxs[:, 0, :])
        tokc = pairs(Wxs[:, 1, 0:F], G)
        kc = pairs(Wxs[:, 1, F:HG], G)
        al = pairs(a2b[:, :], G)
        Pm = sb("Pm", [P, NP2, F])

        s_const = sem("s_const")
        s_tick = sem("s_tick")
        s_clear = sem("s_clear")
        s_zero = sem("s_zero")
        s_edge = sem("s_edge")
        s_zdma = sem("s_zdma")
        s_x = sem("s_x")
        s_w = sem("s_w")
        s_dve = sem("s_dve")
        s_act = sem("s_act")
        s_cnt = sem("s_cnt")
        s_pre = sem("s_pre")
        s_ct = sem("s_ct")
        s_ctc = sem("s_ctc")
        s_slot = sem("s_slot")
        s_stage = sem("s_stage")
        s_scat = [sem(f"s_scat{k}") for k in range(2)]
        s_srec = sem("s_srec")
        s_ti = sem("s_ti")
        s_ge = sem("s_ge")
        s_gs = sem("s_gs")
        s_dec = sem("s_dec")
        s_wxt = sem("s_wxt")
        s_wxc = sem("s_wxc")
        s_wxs = sem("s_wxs")
        s_wxd = sem("s_wxd")
        s_var = sem("s_var")
        s_rs0 = sem("s_rs0")
        s_rs = sem("s_rs")
        s_xn = sem("s_xn")
        s_xt = sem("s_xt")
        s_xc = sem("s_xc")
        s_gm = sem("s_gm")
        s_gx = sem("s_gx")
        s_gt = sem("s_gt")
        s_gd = [sem(f"s_gd{k}") for k in range(2)]
        s_idx = sem("s_idx")
        s_row = [sem(f"s_row{u}") for u in range(2 * U)]
        s_S = sem("s_S")
        s_seg = sem("s_seg")
        s_add = sem("s_add")
        s_rel = sem("s_rel")
        s_neg = sem("s_neg")
        s_ex = sem("s_ex")
        s_px = sem("s_px")
        s_x1 = sem("s_x1")
        s_z1 = sem("s_z1")
        s_l1 = sem("s_l1")
        s_l2 = sem("s_l2")
        s_zs = sem("s_zs")
        s_mz = sem("s_mz")
        s_lm = sem("s_lm")
        s_ls = sem("s_ls")
        s_le = sem("s_le")
        s_sw = sem("s_sw")
        s_wt = sem("s_wt")
        s_wc = sem("s_wc")
        s_M = sem("s_M")
        s_mid = sem("s_mid")
        s_mic = sem("s_mic")
        s_mia = sem("s_mia")
        s_wl = sem("s_wl")
        s_o = sem("s_o")
        s_os = sem("s_os")
        s_od = [sem(f"s_od{k}") for k in range(2)]

        wloads = []
        for k in range(2):
            wloads += [(Wg[:, k, 0:F], W[k * P:(k + 1) * P, :]),
                       (Wxr[:, k, :, :].rearrange("p m f -> p m f"),
                        W_x[k * P:(k + 1) * P, :].rearrange("p (m f) -> p m f", m=2)),
                       (Wfx[:, k, :], W_fx[k * P:(k + 1) * P, :])]
        wloads += [(Wo[:, c, :], W_out[c * P:(c + 1) * P, :]) for c in range(NP2)]
        wloads += [(a1b[:, :], a1.rearrange("f o -> (f o)").partition_broadcast(P)),
                   (a2b[:, :], a2.rearrange("f o -> (f o)").partition_broadcast(P)),
                   (bfx[:, :], b_fx.rearrange("(o n) -> o n", o=1)),
                   (bob[:, :], b_out.partition_broadcast(G)),
                   (tb[:, :], temp.rearrange("a h b c -> (a h b c)").partition_broadcast(P)),
                   (bsr[:, :], b_slice.rearrange("(o n) -> o n", o=1))]
        wloads += [(bxc[:, c:c + 1], b_x[c * P:(c + 1) * P].rearrange("(p o) -> p o", o=1)) for c in range(NP2)]
        for i, w in enumerate((W_slice, W_q, W_k, W_v)):
            wloads += [(W2[0:G, i, 0:G], w), (W2[G:P, i, G:P], w)]
        LAST = NB - 1

        block = ctx.enter_context(nc.Block())

        @block.sync
        def _(sp):
            sp.wait_ge(s_clear, 1)
            for t, a in ((rowi, src), (coli, dst), (ewi, ew.bitcast(I32))):
                sp.dma_start(t[:, 0:ECOL], a[0:P * ECOL].rearrange("(p j) -> p j", p=P)).then_inc(s_edge, 16)
                sp.dma_start(t[0:EREST, ECOL:ECOL + 1],
                             a[P * ECOL:E].rearrange("(p j) -> p j", j=1)).then_inc(s_edge, 16)
            sp.wait_ge(s_clear, 3)
            sp.dma_start(srt.rearrange("(p t) k -> p (t k)", p=P), zero_rec).then_inc(s_zdma, 16)
            sp.dma_start(xs[:, 0:LAST, :], x[0:LAST * P, :].rearrange("(b p) f -> p b f", p=P)).then_inc(s_x, 16)
            sp.dma_start(xs[0:TAIL, LAST, :], x[LAST * P:N, :]).then_inc(s_x, 16)
            sp.wait_ge(s_zero, 1)
            for d, s in wloads:
                sp.dma_start(d, s).then_inc(s_w, 16)

            def store_g(b, k):
                sp.wait_ge(s_gt, b + 1)
                sp.dma_start(gtab[ds(b * P, P), :], Gt[:, k, :]).then_inc(s_gd[k], 16)

            with sp.Fori(0, NB // 2) as i:
                for k in range(2):
                    store_g(i * 2 + k, k)
            store_g(LAST, 0)

            for k in range(2):
                sp.wait_ge(s_scat[k], 16 * EC // 2)
            sp.dma_start(srec, srt.rearrange("(p t) k -> p t k", p=P)).then_inc(s_srec, 16)

            def store_o(b, k, n=P):
                sp.wait_ge(s_os, b + 1)
                sp.dma_start(out[ds(b * P, n), :], pos[0:n, k, :]).then_inc(s_od[k], 16)

            with sp.Fori(0, NB // 2) as i:
                for k in range(2):
                    store_o(i * 2 + k, k)
            store_o(LAST, 0, TAIL)
            sp.wait_ge(s_od[0], 16 * (NB // 2 + 1))
            sp.wait_ge(s_od[1], 16 * (NB // 2))

        @block.gpsimd
        def _(pool):
            pool.iota(iota[:, :], pattern=[[1, P]], base=0, channel_multiplier=0,
                      allow_small_or_imprecise_dtypes=True).then_inc(s_const, 1)
            pool.iota(iotap[:, :], pattern=[[1, 1]], base=0, channel_multiplier=1,
                      allow_small_or_imprecise_dtypes=True).then_inc(s_const, 1)
            pool.iota(slotf[:, ECOL:EC], pattern=[[P, EC - ECOL]], base=P * CAP, channel_multiplier=1,
                      allow_small_or_imprecise_dtypes=True).then_inc(s_const, 1)
            pool.memset(ones[:, :], 1.0).then_inc(s_const, 1)
            pool.memset(onesb[:, :], 1.0).then_inc(s_const, 1)

            pool.wait_ge(s_zdma, 16)
            with pool.Fori(0, EC // (2 * U)) as i:
                for k in range(2):
                    pool.wait_ge(s_stage, i * 2 + k + 1)
                    pool.sem_inc(s_tick, 1)
                    for u in range(U):
                        pool.indirect_dma_start(
                            srt[:, :], bass.IndirectOffsetOnAxis(ap=ring_i[:, k, u:u + 1], axis=0),
                            ring_r[:, k, u, :], None).then_inc(s_scat[k], 16)

            pool.wait_ge(s_slot, 1)
            for k in range(2):
                pool.wait_ge(s_scat[k], 16 * EC // 2)
            pool.iota(iota_t, pattern=[[1, CAP]], base=0, channel_multiplier=0,
                      allow_small_or_imprecise_dtypes=True).then_inc(s_ti, 1)

            pool.wait_ge(s_gd[0], 16 * (NB // 2 + 1))
            pool.wait_ge(s_gd[1], 16 * (NB // 2))

            def gather(i, first):
                for k in range(2):
                    pool.wait_ge(s_idx, i * 2 + k + 1)
                    if not first:
                        pool.wait_ge(s_seg, (i * 2 + k - 1) * U)
                    pool.sem_inc(s_tick, 1)
                    for u in range(U):
                        pool.indirect_dma_start(
                            rows[:, k * U + u, :], None, gtab[:, :],
                            bass.IndirectOffsetOnAxis(ap=ring_i[:, k, u:u + 1], axis=0)).then_inc(s_row[k * U + u], 16)

            gather(0, True)
            with pool.Fori(1, CAP // (2 * U)) as i:
                gather(i, False)

            def add_x(b, k):
                pool.wait_ge(s_rel, b + 1)
                pool.tensor_tensor(pos[:, k, :], pos[:, k, :], xs[:, ds(b, 1), :].rearrange("p o f -> p (o f)"),
                                   ALU.add).then_inc(s_px, 1)

            with pool.Fori(0, NB // 2) as i:
                for k in range(2):
                    add_x(i * 2 + k, k)
            add_x(LAST, 0)

        @block.vector
        def _(dve):
            step = Chain(dve, s_dve)
            v = nc.vector

            v.memset(rowi[:, ECOL:EC], NB * P)
            v.memset(coli[:, ECOL:EC], 0)
            v.memset(ewi[:, ECOL:EC], 0).then_inc(s_clear, 1)
            v.memset(zero_rec, 0).then_inc(s_clear, 1)
            v.memset(xs[:, LAST, :], 0.0).then_inc(s_clear, 1)
            v.memset(W2[:, :, :], 0.0).then_inc(s_zero, 1)
            dve.wait_ge(s_const, 5)
            v.tensor_scalar(ident[:, :], iota[:, :], iotap[:, 0:1], None, ALU.is_equal)
            v.tensor_scalar(lower[:, :], iota[:, :], iotap[:, 0:1], None, ALU.is_gt)
            v.memset(valid[:, :], 1.0)
            step(v.tensor_scalar(padf[:, :], iotap[:, :], float(TAIL), None, ALU.is_ge))
            step(v.tensor_scalar(valid[:, LAST:NB], padf[:, :], -1.0, 1.0, ALU.mult, ALU.add))

            dve.wait_ge(s_edge, 96)
            step(v.tensor_scalar(sloti, rowi, 7, None, ALU.logical_shift_right))
            step(v.tensor_scalar(tmpi, rowi, P - 1, None, ALU.bitwise_and))
            step(v.tensor_copy(hif, sloti))
            v.scalar_tensor_tensor(rec[:, :, 0], coli, 7, tmpi, ALU.logical_shift_left, ALU.bitwise_or)
            v.tensor_copy(rec[:, :, 1], ewi)
            with dve.Fori(0, NB // Q) as i:
                step.enter(i, 0, Q + 1)
                for q in range(Q):
                    step(v.tensor_scalar(scan, hif, iota[:, ds(i * Q + q, 1)], 0.0, ALU.is_equal, ALU.add,
                                         accum_out=part[:, q:q + 1]))
                step(v.tensor_copy(cnt[:, ds(i * Q, Q)], part[:, :]))
            step.leave(NB // Q, Q + 1)
            dve.sem_inc(s_cnt, 1)
            dve.wait_ge(s_pre, 1)
            step(v.tensor_scalar(nti[:, :], bank[0][:, 64:64 + NB], float(P - 1), None, ALU.add))
            step(v.tensor_scalar(nti[:, :], nti[:, :], 7, None, ALU.logical_shift_right))
            step(v.tensor_copy(ntf[:, :], nti[:, :]))
            step(v.tensor_tensor_scan(ctf[:, :], ones[:, 0:NB], ntf[:, :], 0.0, ALU.mult, ALU.add))
            step(v.tensor_tensor(base[:, :], ctf[:, :], ntf[:, :], ALU.subtract))
            step(v.scalar_tensor_tensor(base[:, :], base[:, :], float(P), bank[0][:, 0:NB], ALU.mult, ALU.add))
            v.tensor_scalar(base[:, :], base[:, :], -1.0, None, ALU.add).then_inc(s_ct, 1)
            dve.wait_ge(s_ct, 1)
            with dve.Fori(0, NB) as b:
                step.enter(b, 0, 3)
                step(v.tensor_scalar(mask[:, :], hif, iota[:, ds(b, 1)], None, ALU.is_equal))
                step(v.tensor_tensor_scan(scan, onesb[:, :], mask[:, :], base[:, ds(b, 1)], ALU.mult, ALU.add))
                dve.sem_inc(s_tick, 1)
                step(v.copy_predicated(slotf, mask[:, :], scan))
            step.leave(NB, 3)
            step(v.tensor_copy(sloti, slotf))
            step(v.tensor_scalar(tmpi, sloti, P - 1, None, ALU.bitwise_and))
            step(v.tensor_scalar(sloti, sloti, 7, None, ALU.logical_shift_right))
            step(v.tensor_copy(sf, sloti))
            step(v.scalar_tensor_tensor(slotf, tmpi, float(PITCH), sf, ALU.mult, ALU.add))
            v.tensor_copy(sloti, slotf).then_inc(s_slot, 1)

            dve.wait_ge(s_w, 16 * len(wloads))
            for k in range(2):
                step(v.tensor_tensor_reduce(xn[:, k, :], Wg[:, k, 0:F], a2b[:, :], 1.0, 0.0, ALU.mult, ALU.add,
                                            accum_out=Wg[:, k, F:GW]))
            step(v.tensor_scalar(tb[:, :], tb[:, :], 0.1, 5.0, ALU.max, ALU.min))
            step(v.reciprocal(tb[:, :], tb[:, :]))
            dve.wait_ge(s_wxs, 1)
            tbc = tb[:, :].unsqueeze(2)
            for k in range(2):
                v.tensor_tensor(Wxs[:, k, :].rearrange("p (h g) -> p h g", g=G),
                                bank[4 + k][:, :].rearrange("p (h g) -> p h g", g=G),
                                tbc.broadcast_to([P, H, G]), ALU.mult)
            step(v.tensor_tensor(bxs[:, :].rearrange("p (h g) -> p h g", g=G),
                                 bank[3][0:1, :].rearrange("p (h g) -> p h g", g=G),
                                 bsr[:, :].unsqueeze(1).broadcast_to([1, H, G]), ALU.add))
            v.tensor_tensor(bxs[:, :].rearrange("p (h g) -> p h g", g=G),
                            bxs[:, :].rearrange("p (h g) -> p h g", g=G),
                            tb[0:1, :].unsqueeze(2).broadcast_to([1, H, G]), ALU.mult).then_inc(s_wxd, 1)

            def stats(b, view):
                return v.bn_stats(st6[:, ds(b, 1), :].rearrange("p o s -> p (o s)"), view)

            def norm_stats(first):
                v.tensor_tensor(mean[:, :], st6[:, :, 1], st6[:, :, 4], ALU.add)
                step(v.tensor_tensor(var[:, :], st6[:, :, 1], st6[:, :, 4], ALU.subtract))
                step(v.scalar_tensor_tensor(var[:, :], var[:, :], 0.25, var[:, :], ALU.mult, ALU.mult))
                step(v.tensor_tensor(nwt[:, :], st6[:, :, 2], st6[:, :, 5], ALU.add))
                step(v.scalar_tensor_tensor(var[:, :], nwt[:, :], 1.0 / F, var[:, :], ALU.mult, ALU.add))
                step(v.tensor_scalar(var[:, :], var[:, :], EPS, None, ALU.add))
                v.tensor_scalar(nwt[:, :], var[:, :], 1.0, None, ALU.mult).then_inc(s_var, 1)
                dve.wait_ge(s_rs0, 1 if first else 2)
                step(v.tensor_tensor(nwt[:, :], var[:, :], rstd[:, :], ALU.mult))
                step(v.tensor_tensor(nwt[:, :], nwt[:, :], rstd[:, :], ALU.mult))
                step(v.tensor_scalar(nwt[:, :], nwt[:, :], -0.5, 1.5, ALU.mult, ALU.add))
                step(v.tensor_tensor(rstd[:, :], rstd[:, :], nwt[:, :], ALU.mult))
                v.scalar_tensor_tensor(nmr[:, :], mean[:, :], -0.5, rstd[:, :], ALU.mult, ALU.mult).then_inc(s_rs, 1)

            dve.wait_ge(s_x, 32)
            with dve.Fori(0, NB // Q) as i:
                for q in range(Q):
                    stats(i * Q + q, xs[:, ds(i * Q + q, 1), :].rearrange("p o f -> p (o f)"))
            step(v.tensor_copy(part[:, :], cnt[:, 0:Q]))
            norm_stats(True)
            dve.wait_ge(s_wxs, 1)
            step(v.memset(acc[:, :, :], 0.0))
            v.tensor_copy(acc[:, LAST, F:GW], padf[:, :]).then_inc(s_add, 1)

            def gate(b, k, first):
                dve.wait_ge(s_gx, b + 1)
                step(v.tensor_scalar(sm[:, k, 1:2], sm[:, k, 0:1], 1.0, None, ALU.add))
                if not first:
                    dve.wait_ge(s_gd[k], (b - k) * 8)
                step(v.reciprocal(Gt[:, k, F:GW], sm[:, k, 1:2]))
                v.tensor_scalar(Gt[:, k, 0:F], bank[3 + k][:, 0:F], Gt[:, k, F:GW], None,
                                ALU.mult).then_inc(s_gt, 1)

            gate(0, 0, True)
            gate(1, 1, True)
            with dve.Fori(1, NB // 2) as i:
                step.enter(i, 1, 4)
                for k in range(2):
                    gate(i * 2 + k, k, False)
            step.leave(NB // 2 - 1, 4)
            gate(LAST, 0, False)

            dve.wait_ge(s_ti, 1)
            dve.wait_ge(s_ctc, 1)
            v.tensor_copy(ctcol[:, :], bank[0][0:NB, 128:129]).then_inc(s_ge, 1)
            dve.wait_ge(s_ge, 1)
            v.tensor_scalar(ge[0:NB, :], iota_t[0:NB, :], ctcol[:, 0:1], None, ALU.is_ge).then_inc(s_ge, 1)
            dve.wait_ge(s_srec, 16)
            step(v.tensor_scalar(offi, srec[:, 0:CAP, 0], P - 1, None, ALU.bitwise_and))
            step(v.tensor_copy(lof, offi))
            v.tensor_scalar(colx, srec[:, 0:CAP, 0], 7, None, ALU.logical_shift_right)
            dve.wait_ge(s_gs, 1)
            for c in range(2):
                w = CAP // 2
                step(v.tensor_scalar(ge[0:1, c * w:(c + 1) * w], bank[1 + c][0:1, 0:w], float(LAST), float(GW),
                                     ALU.min, ALU.mult))
            v.tensor_copy(offi[0:1, :], ge[0:1, :]).then_inc(s_dec, 1)
            dve.wait_ge(s_dec, 1)

            def feat(b):
                return acc[:, ds(b, 1), 0:F].rearrange("p o f -> p (o f)")

            accf = acc[:, :, :].rearrange("p b w -> p (b w)")

            def offset(t):
                return v.value_load(offi[0:1, ds(t, 1)], min_val=0, max_val=LAST * GW)

            def select(t, r):
                v.tensor_scalar(S[:, r, :], iota[:, :], lof[:, ds(t, 1)], sewf[:, ds(t, 1), 1],
                                ALU.is_equal, ALU.mult).then_inc(s_S, 1)

            def add(t, r):
                off = offset(t)
                dve.wait_ge(s_seg, t + 1)
                dve.wait_ge(s_add, t + 1)
                a = accf[:, ds(off, GW)]
                v.tensor_tensor(a, a, bank[SEGB[r]][:, 0:GW], ALU.add).then_inc(s_add, 1)

            for r in range(4):
                select(r, r)
            with dve.Fori(0, CAP // 4 - 1) as i:
                for r in range(4):
                    add(i * 4 + r, r)
                    select(i * 4 + r + 4, r)
            for r in range(4):
                add(CAP - 4 + r, r)
            dve.wait_ge(s_add, CAP + 1)

            v.memset(zrow[:, :], 0.0).then_inc(s_zs, 1)
            step(v.reciprocal(rinv[:, :], acc[:, :, F]))
            with dve.Fori(0, NB // Q) as i:
                step.enter(i, 0, Q + 1)
                for q in range(Q):
                    step(v.scalar_tensor_tensor(neg[:, 0, :], feat(i * Q + q), 1.0, a1b[:, :], ALU.mult, ALU.mult,
                                                accum_out=part[:, q:q + 1]))
                step(v.tensor_copy(zd[:, ds(i * Q, Q)], part[:, :]))
            step.leave(NB // Q, Q + 1)
            step(v.tensor_tensor(zd[:, :], zd[:, :], rinv[:, :], ALU.mult))
            v.scalar_tensor_tensor(za[:, :], zd[:, :], -1.0, zd[:, :], ALU.mult, ALU.min).then_inc(s_z1, 1)
            dve.wait_ge(s_l1, 2)
            v.scalar_tensor_tensor(ld[:, :], zd[:, :], 0.0, za[:, :], ALU.max, ALU.add).then_inc(s_l2, 1)

            def negative(b, k, first):
                if not first:
                    dve.wait_ge(s_x1, b - 1)
                v.tensor_scalar(neg[:, k, :], feat(b), rinv[:, ds(b, 1)], 0.0, ALU.mult, ALU.min).then_inc(s_neg, 1)

            def finish(b, k):
                dve.wait_ge(s_ex, b + 1)
                dve.wait_ge(s_px, b + 1)
                v.scalar_tensor_tensor(feat(b), neg[:, k, :], -1.0, pos[:, k, :], ALU.add, ALU.add).then_inc(s_x1, 1)
                dve.wait_ge(s_x1, b + 1)
                dve.sem_inc(s_tick, 1)
                step(stats(b, feat(b)))

            negative(0, 0, True)
            negative(1, 1, True)
            with dve.Fori(0, NB // 2 - 1) as i:
                step.enter(i, 0, 2)
                for k in range(2):
                    finish(i * 2 + k, k)
                    negative(i * 2 + k + 2, k, False)
            step.leave(NB // 2 - 1, 2)
            finish(NB - 3, 0)
            negative(LAST, 0, False)
            finish(NB - 2, 1)
            finish(LAST, 0)
            norm_stats(False)

            def heads(t):
                return t.rearrange("p (h g) -> p h g", g=G)

            def shift(b, k, first):
                dve.wait_ge(s_lm, b + 1)
                step(v.tensor_reduce(hm[:, k, 0, :], heads(bank[4 + k][:, :]), AX.X, ALU.max))
                if not first:
                    dve.wait_ge(s_sw, b - 1)
                v.tensor_tensor(heads(lg[:, k, :]), heads(bank[4 + k][:, :]),
                                hm[:, k, 0, :].unsqueeze(2).broadcast_to([P, H, G]), ALU.subtract).then_inc(s_ls, 1)

            def weigh(b, k, first):
                dve.wait_ge(s_le, b + 1)
                step(v.tensor_reduce(hm[:, k, 1, :], heads(lg[:, k, :]), AX.X, ALU.add))
                step(v.reciprocal(hm[:, k, 2, :], hm[:, k, 1, :]))
                if not first:
                    dve.wait_ge(s_M, b - 1)
                v.tensor_tensor(heads(sw[:, k, :]), heads(lg[:, k, :]),
                                hm[:, k, 2, :].unsqueeze(2).broadcast_to([P, H, G]), ALU.mult).then_inc(s_sw, 1)

            shift(0, 0, True)
            weigh(0, 0, True)
            shift(1, 1, True)
            weigh(1, 1, True)
            with dve.Fori(1, NB // 2) as i:
                step.enter(i, 1, 6)
                for k in range(2):
                    shift(i * 2 + k, k, False)
                    weigh(i * 2 + k, k, False)
            step.leave(NB // 2 - 1, 6)
            shift(LAST, 0, False)
            weigh(LAST, 0, False)

            dve.wait_ge(s_M, NB)
            for t in (tokd, qd, vd, ad):
                v.memset(t[:, :, :], 0.0)
            step(v.tensor_scalar(nrm[:, 0, :], bank[2][:, 0:NP2], 1e-5, None, ALU.add))
            step(v.reciprocal(nrm[:, 1, :], nrm[:, 0, :]))
            step(v.tensor_tensor(nrm[:, 2, :], bank[2][:, 0:NP2], nrm[:, 1, :], ALU.mult))
            for c in range(NP2):
                m = v.tensor_scalar(Mn[:, c, :], bank[c // 2][:, (c % 2) * F:(c % 2 + 1) * F], nrm[:, 1, c:c + 1], None,
                                    ALU.mult)
            m.then_inc(s_mic, 1)
            mid = [0]

            def waitmid():
                mid[0] += 1
                dve.wait_ge(s_mid, mid[0])

            waitmid()
            v.tensor_copy(MnT[:, 0, :], bank[4][:, :])
            v.tensor_copy(MnT[:, 1, :], bank[5][:, :])
            v.tensor_copy(nbT[:, :], bank[6][0:1, :]).then_inc(s_mic, 1)

            def halves(dst, psum, last=None):
                w = psum.rearrange("p (c n) -> p c n", n=P)
                v.tensor_copy(dst[0:G, :, 0:G], w[0:G, :, 0:G])
                return v.tensor_copy(dst[G:P, :, G:P], w[G:P, :, G:P])

            waitmid()
            halves(tokd, bank[7][:, :])
            w7 = bank[7][:, :].rearrange("p (c n) -> p c n", n=P)
            v.tensor_copy(tokc[0:G, :, :], w7[0:G, :, 0:G])
            v.tensor_copy(tokc[G:P, :, :], w7[G:P, :, G:P]).then_inc(s_mic, 1)
            waitmid()
            halves(qd, bank[4][:, :])
            v.tensor_copy(kc[:, :, :], bank[5][:, 0:NP2 * G].rearrange("p (c n) -> p c n", n=G))
            halves(vd, bank[6][:, :]).then_inc(s_mic, 1)
            waitmid()
            sc = bank[7][:, 0:NP2 * G].rearrange("p (c n) -> p c n", n=G)
            step(v.tensor_reduce(nrm[:, 0, :], sc, AX.X, ALU.max))
            v.tensor_tensor(al[:, :, :], sc, nrm[:, 0, :].unsqueeze(2).broadcast_to([P, NP2, G]),
                            ALU.subtract).then_inc(s_mic, 1)
            dve.wait_ge(s_mia, 1)
            step(v.tensor_reduce(nrm[:, 1, :], al[:, :, :], AX.X, ALU.add))
            step(v.reciprocal(nrm[:, 2, :], nrm[:, 1, :]))
            for lo in (0, G):
                m = v.tensor_tensor(ad[lo:lo + G, :, lo:lo + G], al[lo:lo + G, :, :],
                                    nrm[lo:lo + G, 2, :].unsqueeze(2).broadcast_to([G, NP2, G]), ALU.mult)
            m.then_inc(s_mic, 1)
            waitmid()
            v.tensor_copy(aT[:, :, :], bank[4][:, :].rearrange("p (c n) -> p c n", n=P)).then_inc(s_mic, 1)
            waitmid()
            v.tensor_copy(oT[:, :, :], bank[5][:, :].rearrange("p (c n) -> p c n", n=P)).then_inc(s_mic, 1)
            waitmid()
            for c in range(NP2):
                m = v.tensor_copy(Pm[:, c, :], bank[6 + c // 2][:, (c % 2) * F:(c % 2 + 1) * F])
            step(m)
            v.tensor_tensor(Pm[0:G, 0, :], Pm[0:G, 0, :], bob[:, :], ALU.add).then_inc(s_mic, 1)

            def result(b, k, first):
                dve.wait_ge(s_o, b + 1)
                if not first:
                    dve.wait_ge(s_od[k], (b - k) * 8)
                v.tensor_tensor(pos[:, k, :], bank[4 + k][:, 0:F], feat(b), ALU.add).then_inc(s_os, 1)

            result(0, 0, True)
            result(1, 1, True)
            with dve.Fori(1, NB // 2) as i:
                for k in range(2):
                    result(i * 2 + k, k, False)
            result(LAST, 0, False)

        @block.scalar
        def _(act):
            a = nc.scalar
            a.preload_act_table_set("natural_log_exp_and_others")
            step = Chain(act, s_act)

            for k in range(2):
                act.wait_ge(s_wxt, k + 1)
                a.copy(WxT[:, :, k * P:(k + 1) * P], bank[6 + k][:, :].rearrange("p (c n) -> p c n", n=P)).then_inc(s_wxc, 1)

            act.wait_ge(s_slot, 1)
            def stage(i, k, first):
                if not first:
                    act.wait_ge(s_scat[k], i * 16 * U)
                a.copy(ring_i[:, k, :], sloti[:, ds((i * 2 + k) * U, U)])
                a.copy(ring_r[:, k, :, :], rec[:, ds((i * 2 + k) * U, U), :]).then_inc(s_stage, 1)

            for k in range(2):
                stage(0, k, True)
            with act.Fori(1, EC // (2 * U)) as i:
                for k in range(2):
                    stage(i, k, False)

            def guess(n):
                act.wait_ge(s_var, n)
                step(a.activation(lnv[:, :], nwt[:, :], ACT.Ln))
                a.activation(rstd[:, :], lnv[:, :], ACT.Exp, scale=-0.5).then_inc(s_rs0, 1)

            guess(1)
            act.wait_ge(s_rs, 1)

            def normalize(b, k, view):
                a.activation(xn[:, k, :], view, ACT.Identity, bias=nmr[:, ds(b, 1)],
                             scale=rstd[:, ds(b, 1)]).then_inc(s_xn, 1)

            def stage1(b, k, first):
                if not first:
                    act.wait_ge(s_xt, b - 1)
                normalize(b, k, xs[:, ds(b, 1), :].rearrange("p o f -> p (o f)"))
                act.wait_ge(s_xt, b + 1)
                if not first:
                    act.wait_ge(s_gm, b - 1)
                a.copy(xT[:, k, :], bank[6 + k][:, 0:F]).then_inc(s_xc, 1)
                act.wait_ge(s_gm, b + 1)
                if not first:
                    act.wait_ge(s_gt, b - 1)
                a.activation(sm[:, k, 0:1], bank[3 + k][:, F:GW], ACT.Exp, scale=-1.0).then_inc(s_gx, 1)

            stage1(0, 0, True)
            stage1(1, 1, True)
            with act.Fori(1, NB // 2) as i:
                for k in range(2):
                    stage1(i * 2 + k, k, False)
            stage1(LAST, 0, False)

            act.wait_ge(s_dec, 1)

            def indices(i, k, first):
                if not first:
                    for u in range(U):
                        act.wait_ge(s_row[k * U + u], i * 16)
                a.copy(ring_i[:, k, :], colx[:, ds((i * 2 + k) * U, U)]).then_inc(s_idx, 1)

            for k in range(2):
                indices(0, k, True)
            with act.Fori(1, CAP // (2 * U)) as i:
                for k in range(2):
                    indices(i, k, False)

            act.wait_ge(s_z1, 1)
            a.activation(nwt[:, :], za[:, :], ACT.Exp).then_inc(s_l1, 1)
            act.wait_ge(s_l1, 1)
            a.activation(za[:, :], nwt[:, :], ACT.Ln, bias=1.0).then_inc(s_l1, 1)
            act.wait_ge(s_l2, 1)

            def parts(b, k, first):
                if not first:
                    act.wait_ge(s_x1, b - 1)
                a.activation(pos[:, k, :], acc[:, ds(b, 1), 0:F].rearrange("p o f -> p (o f)"), ACT.Relu,
                             scale=rinv[:, ds(b, 1)]).then_inc(s_rel, 1)
                act.wait_ge(s_neg, b + 1)
                a.activation(neg[:, k, :], neg[:, k, :], ACT.Exp, scale=ld[:, ds(b, 1)]).then_inc(s_ex, 1)

            parts(0, 0, True)
            parts(1, 1, True)
            with act.Fori(1, NB // 2) as i:
                for k in range(2):
                    parts(i * 2 + k, k, False)
            parts(LAST, 0, False)
            guess(2)
            act.wait_ge(s_rs, 2)

            def stage2(b, k, first):
                if not first:
                    act.wait_ge(s_M, b - 1)
                normalize(b, k, acc[:, ds(b, 1), 0:F].rearrange("p o f -> p (o f)"))
                act.wait_ge(s_xt, NB + b + 1)
                if not first:
                    act.wait_ge(s_lm, b - 1)
                a.copy(xT[:, k, :], bank[3][:, k * F:(k + 1) * F]).then_inc(s_xc, 1)
                act.wait_ge(s_ls, b + 1)
                a.activation(lg[:, k, :], lg[:, k, :], ACT.Exp).then_inc(s_le, 1)

            def keep(b, k):
                act.wait_ge(s_wt, b + 1)
                a.copy(swt[:, :, ds(b * P, P)], bank[6 + k][:, :].rearrange("p (c n) -> p c n", n=P)).then_inc(s_wc, 1)

            stage2(0, 0, True)
            stage2(1, 1, True)
            keep(0, 0)
            with act.Fori(1, NB // 2) as i:
                for k in range(2):
                    stage2(i * 2 + k, k, False)
                    keep(i * 2 + k - 1, 1 - k)
            stage2(LAST, 0, False)
            keep(LAST - 1, 1)
            keep(LAST, 0)

            act.wait_ge(s_mic, 5)
            a.activation(al[:, :, :], al[:, :, :], ACT.Exp, scale=SCALE).then_inc(s_mia, 1)

            act.wait_ge(s_mic, 9)
            def load(b, k, first):
                if not first:
                    act.wait_ge(s_o, b - 1)
                a.copy(lg[:, k, :].rearrange("p (c n) -> p c n", n=P), swt[:, :, ds(b * P, P)]).then_inc(s_wl, 1)

            load(0, 0, True)
            load(1, 1, True)
            with act.Fori(1, NB // 2) as i:
                for k in range(2):
                    load(i * 2 + k, k, False)
            load(LAST, 0, False)

        @block.tensor
        def _(pe):
            def mm(o, l, r, start=True, stop=True):
                return nc.tensor.matmul(o, l, r, start=start, stop=stop, skip_group_check=True)

            pe.wait_ge(s_w, 16 * len(wloads))
            pe.wait_ge(s_dve, 2)
            for k in range(2):
                for c in range(NP2):
                    t = nc.tensor.transpose(bank[6 + k][:, c * P:(c + 1) * P], Wxr[:, k, c // 2, (c % 2) * P:(c % 2 + 1) * P], ident[:, :])
                t.then_inc(s_wxt, 1)
            pe.wait_ge(s_wxc, 2)
            for c in range(NP2):
                for k in range(2):
                    mm(bank[4 + k][:, c * P:(c + 1) * P], WxT[:, c, k * P:(k + 1) * P], W2[:, 0, :])
                m = mm(bank[3][0:1, c * P:(c + 1) * P], bxc[:, c:c + 1], W2[:, 0, :])
            m.then_inc(s_wxs, 1)

            pe.wait_ge(s_cnt, 1)
            mm(bank[0][:, 0:NB], lower[:, :], cnt[:, :])
            mm(bank[0][:, 64:64 + NB], ones[:, :], cnt[:, :]).then_inc(s_pre, 1)
            pe.wait_ge(s_ct, 1)
            mm(bank[0][0:NB, 128:129], ctf[0:1, :], ones[0:1, 0:1]).then_inc(s_ctc, 1)

            pe.wait_ge(s_wxd, 1)
            def transposes(n, k, b, ps):
                pe.wait_ge(s_xn, n + 1)
                for c in range(2):
                    t = nc.tensor.transpose(ps[:, c * P:(c + 1) * P], xn[:, k, c * P:(c + 1) * P], ident[:, :])
                t.then_inc(s_xt, 1)

            def support(b, k, first):
                if not first:
                    pe.wait_ge(s_xc, b - 1)
                transposes(b, k, b, bank[6 + k])
                pe.wait_ge(s_xc, b + 1)
                if not first:
                    pe.wait_ge(s_gt, b - 1)
                mm(bank[3 + k][:, 0:GW], xT[:, k, 0:P], Wg[:, 0, :], True, False)
                mm(bank[3 + k][:, 0:GW], xT[:, k, P:F], Wg[:, 1, :], False, True).then_inc(s_gm, 1)

            support(0, 0, True)
            support(1, 1, True)
            with pe.Fori(1, NB // 2) as i:
                for k in range(2):
                    support(i * 2 + k, k, False)
            support(LAST, 0, False)

            pe.wait_ge(s_ge, 2)
            for c in range(2):
                w = CAP // 2
                m = mm(bank[1 + c][0:1, 0:w], ones[0:NB, 0:1], ge[0:NB, c * w:(c + 1) * w])
            m.then_inc(s_gs, 1)
            pe.wait_ge(s_dec, 1)

            def segment(i, first):
                for u in range(2 * U):
                    t = i * 2 * U + u
                    pe.wait_ge(s_row[u], i * 16 + 16)
                    pe.wait_ge(s_S, t + 1)
                    if not first or u >= 4:
                        pe.wait_ge(s_add, t - 2)
                    mm(bank[SEGB[u % 4]][:, 0:GW], S[:, u % 4, :], rows[:, u, :]).then_inc(s_seg, 1)

            segment(0, True)
            with pe.Fori(1, CAP // (2 * U)) as i:
                segment(i, False)

            pe.wait_ge(s_zs, 1)
            pe.wait_ge(s_add, CAP + 1)
            for c in range(3):
                m = mm(bank[c][:, :], zrow[0:1, 0:P], zrow[0:1, :], True, False)
            m.then_inc(s_mz, 1)

            def logits(b, k, first):
                if not first:
                    pe.wait_ge(s_xc, NB + b - 1)
                transposes(NB + b, k, b, bank[3][:, k * F:(k + 1) * F])
                if not first:
                    pe.wait_ge(s_ls, b - 1)
                mm(bank[4 + k][:, :], ones[0:1, :], bxs[:, :], True, False)
                pe.wait_ge(s_xc, NB + b + 1)
                mm(bank[4 + k][:, :], xT[:, k, 0:P], Wxs[:, 0, :], False, False)
                mm(bank[4 + k][:, :], xT[:, k, P:F], Wxs[:, 1, :], False, True).then_inc(s_lm, 1)

            def sums(b, k, first):
                pe.wait_ge(s_sw, b + 1)
                if not first:
                    pe.wait_ge(s_wc, b - 1)
                for c in range(NP2):
                    t = nc.tensor.transpose(bank[6 + k][:, c * P:(c + 1) * P], sw[:, k, c * P:(c + 1) * P], ident[:, :])
                t.then_inc(s_wt, 1)
                for c in range(NP2):
                    w = sw[:, k, c * P:(c + 1) * P]
                    mm(bank[c // 2][:, (c % 2) * F:(c % 2 + 1) * F], w, xn[:, k, :], False, False)
                    m = mm(bank[2][:, c:c + 1], w, valid[:, ds(b, 1)], False, False)
                m.then_inc(s_M, 1)

            logits(0, 0, True)
            logits(1, 1, True)
            sums(0, 0, True)
            logits(2, 0, False)
            sums(1, 1, True)
            with pe.Fori(1, NB // 2 - 1) as i:
                for k in range(2):
                    logits(i * 2 + k + 1, 1 - k, False)
                    sums(i * 2 + k, k, False)
            logits(LAST - 1, 1, False)
            sums(LAST - 2, 0, False)
            logits(LAST, 0, False)
            sums(LAST - 1, 1, False)
            sums(LAST, 0, False)

            mic = [0]

            def waitmic(n=1):
                mic[0] += n
                pe.wait_ge(s_mic, mic[0])

            pe.wait_ge(s_wc, NB)
            waitmic()
            for c in range(NP2):
                for f in range(2):
                    nc.tensor.transpose(bank[4 + f][:, c * P:(c + 1) * P], Mn[:, c, f * P:(f + 1) * P], ident[:, :])
                t = nc.tensor.transpose(bank[6][0:1, c * P:(c + 1) * P], nrm[:, 2, c:c + 1], ident[:, :])
            t.then_inc(s_mid, 1)
            waitmic()
            for c in range(NP2):
                o = bank[7][:, c * P:(c + 1) * P]
                cs = slice(c * P, (c + 1) * P)
                mm(o, Wfx[:, 0, cs], MnT[:, 0, cs], True, False)
                mm(o, Wfx[:, 1, cs], MnT[:, 1, cs], False, False)
                m = mm(o, bfx[:, cs], nbT[:, cs], False, True)
            m.then_inc(s_mid, 1)
            waitmic()
            for c in range(NP2):
                mm(bank[4][:, c * P:(c + 1) * P], W2[:, 1, :], tokd[:, c, :])
                mm(bank[5][:, c * G:(c + 1) * G], W2[:, 2, :], tokc[:, c, :])
                m = mm(bank[6][:, c * P:(c + 1) * P], tokd[:, c, :], W2[:, 3, :])
            m.then_inc(s_mid, 1)
            waitmic()
            for c in range(NP2):
                m = mm(bank[7][:, c * G:(c + 1) * G], qd[:, c, :], kc[:, c, :])
            m.then_inc(s_mid, 1)
            waitmic(2)
            for c in range(NP2):
                t = nc.tensor.transpose(bank[4][:, c * P:(c + 1) * P], ad[:, c, :], ident[:, :])
            t.then_inc(s_mid, 1)
            waitmic()
            for c in range(NP2):
                m = mm(bank[5][:, c * P:(c + 1) * P], vd[:, c, :], aT[:, c, :])
            m.then_inc(s_mid, 1)
            waitmic()
            for c in range(NP2):
                m = mm(bank[6 + c // 2][:, (c % 2) * F:(c % 2 + 1) * F], oT[:, c, :], Wo[:, c, :])
            m.then_inc(s_mid, 1)
            waitmic()

            def product(b, k, first):
                pe.wait_ge(s_wl, b + 1)
                if not first:
                    pe.wait_ge(s_os, b - 1)
                for c in range(NP2):
                    m = mm(bank[4 + k][:, 0:F], lg[:, k, c * P:(c + 1) * P], Pm[:, c, :], c == 0, c == NP2 - 1)
                m.then_inc(s_o, 1)

            product(0, 0, True)
            product(1, 1, True)
            with pe.Fori(1, NB // 2) as i:
                for k in range(2):
                    product(i * 2 + k, k, False)
            product(LAST, 0, False)


_INS = ['x', 'src', 'dst', 'edge_weight', 'L0_gnn_W', 'L0_gnn_a1', 'L0_gnn_a2', 'L0_ffn_W_fx', 'L0_ffn_b_fx',
        'L0_ffn_W_x', 'L0_ffn_b_x', 'L0_ffn_W_slice', 'L0_ffn_b_slice', 'L0_ffn_W_q', 'L0_ffn_W_k', 'L0_ffn_W_v',
        'L0_ffn_W_out', 'L0_ffn_b_out', 'L0_ffn_temperature']


def kernel(**inputs):
    import numpy as _np
    import concourse.bacc as _bacc
    from concourse import mybir as _mybir
    from concourse.bass_utils import run_bass_kernel_spmd as _run

    nc = _bacc.Bacc("TRN2", target_bir_lowering=False, num_devices=1)
    arrays, args = {}, []
    for name in _INS:
        a = _np.ascontiguousarray(inputs[name])
        arrays[f"in_{name}_dram"] = a
        args.append(nc.dram_tensor(f"in_{name}_dram", a.shape, _mybir.dt.from_np(a.dtype), kind="ExternalInput").ap())
    out = nc.dram_tensor("out_0_dram", (N, F), F32, kind="ExternalOutput").ap()
    gtab = nc.dram_tensor("gated_rows_dram", (NB * P, GW), F32, kind="Internal").ap()
    srt = nc.dram_tensor("sorted_edges_dram", (P * PITCH, 2), I32, kind="Internal").ap()
    build(nc, *args, out, gtab, srt)
    r = _run(nc, [arrays], core_ids=[0])
    return r.results[0]["out_0_dram"]
```

```python
import numpy as np
from contextlib import ExitStack

import concourse.bass as bass
from concourse import mybir

F32 = mybir.dt.float32
BF16 = mybir.dt.bfloat16
I32 = mybir.dt.int32
U8 = mybir.dt.uint8
ALU = mybir.AluOpType
ACT = mybir.ActivationFunctionType
AX = mybir.AxisListType

P = 128
N = 6250
F = 256
E = 106250
NB = -(-N // P)
TAIL = N - (NB - 1) * P
ECOL = E // P
EREST = E - ECOL * P
EC = 832
TQ = 19
T = NB * TQ
OV = -(-(E // P + NB) // 2) * 2
PITCH = T + OV + EC - ECOL
UG = (5, 10, 15, TQ)
AH = 9
H = 8
G = 64
D = 64
HG = H * G
NP2 = H // 2
GW = F + 1
U = 8
Q = 7
assert NB % Q == 0
EPS = 1e-5
SCALE = float(D) ** -0.5
ds = bass.ds


class Chain:

    def __init__(self, eng, sem):
        self.eng, self.sem, self.n, self.loop, self.per = eng, sem, 0, 0, 0

    def __call__(self, ins):
        ins.then_inc(self.sem, 1)
        self.n += 1
        self.eng.wait_ge(self.sem, self.loop + self.n)
        return self

    def enter(self, i, first, per):
        self.loop = (i - first) * per

    def leave(self, count, per):
        self.loop = 0
        self.n += (count - 1) * per


def build(nc, x, src, dst, ew, W, a1, a2, W_fx, b_fx, W_x, b_x, W_slice, b_slice, W_q, W_k, W_v,
          W_out, b_out, temp, out, gtab, srt, ovs):
    with ExitStack() as ctx:
        def sb(name, shape, dt=F32):
            return ctx.enter_context(nc.sbuf_tensor(name, shape, dt))

        def sem(name):
            return ctx.enter_context(nc.semaphore(name))

        bank = [ctx.enter_context(nc.psum_tensor(f"bank{i}", [P, 512], F32)) for i in range(8)]

        res = sb("res", [P, NB, F])
        big = sb("big", [P, 4 * NB * P])
        swt = big[:, :].rearrange("p (c n) -> p c n", c=4)
        acc = big[:, 0:NB * GW].rearrange("p (b w) -> p b w", b=NB)
        accf = big[:, 0:NB * GW]
        srec = sb("srec", [P, T, 2], I32)
        sewf = srec[:, :, :].rearrange("p t k -> p (t k)").bitcast(F32).rearrange("p (t k) -> p t k", k=2)
        rows_t = sb("rows", [P, TQ * GW])
        rows = rows_t[:, :].rearrange("p (u w) -> p u w", w=GW)
        S_t = sb("S", [P, TQ * P])
        S = S_t[:, :].rearrange("p (u r) -> p u r", r=P)

        class Carve:

            def __init__(self, t, at, end):
                self.t, self.at, self.end = t, at, end

            def __call__(self, n, dt=F32):
                v = self.t[:, self.at:self.at + n]
                self.at += n
                assert self.at <= self.end
                return v if dt == F32 else v.bitcast(dt)

        carve = Carve(big, NB * GW, 4 * NB * P)
        rowi = carve(EC, I32)
        coli = carve(EC, I32)
        ewi = carve(EC, I32)
        rec = carve(2 * EC, I32).rearrange("p (j k) -> p j k", k=2)
        hif = carve(EC)
        slotf = carve(EC)
        scan = carve(EC)
        sf = carve(EC)
        sloti = carve(EC, I32)
        tmpi = carve(EC, I32)
        zero_rec = carve(PITCH, I32)
        cnt, ntf, ctf, base = carve(NB), carve(NB), carve(NB), carve(NB)
        nti = carve(NB, I32)
        first = carve(NB)
        limit = carve(NB)
        jump = carve(NB)
        st6 = carve(6 * NB).rearrange("p (b s) -> p b s", s=6)
        mean = carve(NB)
        var, lnv, rstd, nmr, nwt = carve(NB), carve(NB), carve(NB), carve(NB), carve(NB)
        carve = Carve(rows_t, 0, TQ * GW)
        mask = carve(EC // 4, U8)
        onesb = carve(EC // 2, BF16)
        lower = carve(P)
        carve = Carve(rows_t, 0, TQ * GW)
        offi = carve(OV, I32)
        iota_t = carve(OV)
        ge = carve(OV)
        orec = carve(2, I32)
        oidx = carve(1, I32)
        olo = carve(2, I32)
        olof = carve(1)
        orow = carve(GW)
        oS = carve(P)
        oewf = orec.bitcast(F32)
        carve = Carve(S_t, 0, TQ * P)
        Wg = carve(2 * GW).rearrange("p (k w) -> p k w", k=2)
        Gt = carve(2 * GW).rearrange("p (k w) -> p k w", k=2)
        a2b = carve(F)
        xn1 = carve(2 * F).rearrange("p (k f) -> p k f", k=2)
        xT1 = carve(2 * F).rearrange("p (k f) -> p k f", k=2)
        carve = Carve(rows_t, 0, TQ * GW)
        Wfx = carve(2 * HG).rearrange("p (k n) -> p k n", k=2)
        Wo = carve(NP2 * F).rearrange("p (c f) -> p c f", f=F)
        Pm = carve(NP2 * F).rearrange("p (c f) -> p c f", f=F)
        bfx = carve(HG)[0:1, :]
        nbT = carve(HG)[0:1, :]
        bob = carve(F)[0:G, :]
        W3 = carve(3 * P).rearrange("p (i n) -> p i n", n=P)
        carve = Carve(S_t, 0, TQ * P)
        stg = carve(2 * HG).rearrange("p (k n) -> p k n", k=2)
        ot = carve(2 * F).rearrange("p (k f) -> p k f", k=2)
        iota = sb("iota", [P, P])
        iotap = sb("iotap", [P, 1])
        ident = sb("ident", [P, P])
        ones = sb("ones", [P, P])
        valid = sb("valid", [P, NB])
        padf = sb("padf", [P, 1])
        a1b = sb("a1b", [P, F])
        Wxs = sb("Wxs", [P, 2, HG])
        bxs = sb("bxs", [1, HG])
        zrow = sb("zrow", [1, P])
        Ws2 = sb("Ws2", [P, P])
        tb = sb("tb", [P, H])
        bsr = sb("bsr", [1, G])
        bxc = sb("bxc", [P, NP2])
        Wxr = srec[:, 0:512, :].rearrange("p t k -> p (t k)").bitcast(F32).rearrange("p (k m f) -> p k m f", k=2, m=2)
        WxT = rows_t[:, 2048:2048 + 1024].rearrange("p (c f) -> p c f", f=F)
        novi = sb("novi", [1, 1], I32)
        ctcol = sb("ctcol", [NB, 1])
        part = sb("part", [P, Q])
        sm = sb("sm", [P, 2, 4])
        hm = sb("hm", [P, 3, H])
        RI, ZD, ZA, EX, LG, LD, VA, LV, RS, NW, NM = range(11)
        bc = sb("bc", [P, 11])
        bst = sb("bst", [P, 6])
        bmv = sb("bmv", [P, 2])

        def col(n):
            return bc[:, n:n + 1]

        ring_s = sb("ring_s", [P, 2, U], I32)
        ring_r = sb("ring_r", [P, 2, U, 2], I32)
        ring_i = sb("ring_i", [P, 2, TQ], I32)
        loi = sb("loi", [P, TQ], I32)
        lof = sb("lof", [P, 2, TQ])
        ovr = sb("ovr", [P, 2, GW])
        ag = sb("ag", [P, GW])
        xn = sb("xn", [P, F])
        xT = sb("xT", [P, F])
        pos = sb("pos", [P, F])
        neg = sb("neg", [P, F])
        lg = sb("lg", [P, HG])
        sw = sb("sw", [P, HG])

        def pairs(t, n=P):
            return t.rearrange("p (c n) -> p c n", n=n)

        MnT = S_t[:, 0:2 * HG].rearrange("p (k n) -> p k n", k=2)
        Mn = S_t[:, 2 * HG:4 * HG].rearrange("p (c f) -> p c f", f=F)
        tokc = pairs(S_t[:, 4 * HG:4 * HG + F], G)
        srf = srec[:, :, :].rearrange("p t k -> p (t k)").bitcast(F32)
        tokd = pairs(srf[:, 0:HG])
        qd = pairs(srf[:, HG:2 * HG])
        vd = pairs(srf[:, 2 * HG:3 * HG])
        kc = pairs(srf[:, 3 * HG:3 * HG + F], G)
        ad = pairs(Wxs[:, 0, :])
        aT = pairs(Wxs[:, 1, :])
        oT = pairs(lg[:, :])
        al = pairs(sw[:, 0:F], G)
        nrm = sb("nrm", [P, 3, NP2])

        s_const = sem("s_const")
        s_tick = sem("s_tick")
        s_clear = sem("s_clear")
        s_zero = sem("s_zero")
        s_edge = sem("s_edge")
        s_zdma = sem("s_zdma")
        s_x = sem("s_x")
        s_w = sem("s_w")
        s_dve = sem("s_dve")
        s_act = sem("s_act")
        s_cnt = sem("s_cnt")
        s_pre = sem("s_pre")
        s_ctc = sem("s_ctc")
        s_slot = sem("s_slot")
        s_stage = sem("s_stage")
        s_scat = [sem(f"s_scat{k}") for k in range(2)]
        s_srec = sem("s_srec")
        s_ti = sem("s_ti")
        s_ge = sem("s_ge")
        s_gs = sem("s_gs")
        s_dja = sem("s_dja")
        s_nov = sem("s_nov")
        s_off = sem("s_off")
        s_orec = sem("s_orec")
        s_oidx = sem("s_oidx")
        s_orow = sem("s_orow")
        s_oS = sem("s_oS")
        s_oseg = sem("s_oseg")
        s_oadd = sem("s_oadd")
        s_ovd = sem("s_ovd")
        s_ovs = sem("s_ovs")
        s_ov = [sem(f"s_ov{k}") for k in range(2)]
        s_ev = sem("s_ev")
        s_wxt = sem("s_wxt")
        s_wxc = sem("s_wxc")
        s_wxs = sem("s_wxs")
        s_wxd = sem("s_wxd")
        s_var = sem("s_var")
        s_rs0 = sem("s_rs0")
        s_rs = sem("s_rs")
        s_xn = sem("s_xn")
        s_xt = sem("s_xt")
        s_xc = sem("s_xc")
        s_gm = sem("s_gm")
        s_gx = sem("s_gx")
        s_gt = sem("s_gt")
        s_gd = [sem(f"s_gd{k}") for k in range(2)]
        s_idx = sem("s_idx")
        s_row = [sem(f"s_row{u}") for u in range(TQ)]
        s_S = sem("s_S")
        s_seg = sem("s_seg")
        s_rel = sem("s_rel")
        s_ex = sem("s_ex")
        s_x1 = sem("s_x1")
        s_w3z = sem("s_w3z")
        s_w3 = sem("s_w3")
        s_z1 = sem("s_z1")
        s_l1 = sem("s_l1")
        s_l2 = sem("s_l2")
        s_zs = sem("s_zs")
        s_mz = sem("s_mz")
        s_lm = sem("s_lm")
        s_ls = sem("s_ls")
        s_le = sem("s_le")
        s_sw = sem("s_sw")
        s_wt = sem("s_wt")
        s_wc = sem("s_wc")
        s_M = sem("s_M")
        s_mid = sem("s_mid")
        s_mic = sem("s_mic")
        s_mia = sem("s_mia")
        s_wl = sem("s_wl")
        s_o = sem("s_o")
        s_os = sem("s_os")
        s_od = [sem(f"s_od{k}") for k in range(2)]

        wloads = []
        for k in range(2):
            wloads += [(Wg[:, k, 0:F], W[k * P:(k + 1) * P, :]),
                       (Wxr[:, k, :, :], W_x[k * P:(k + 1) * P, :].rearrange("p (m f) -> p m f", m=2)),
                       (Ws2[k * G:(k + 1) * G, k * G:(k + 1) * G], W_slice)]
        wloads += [(a1b[:, :], a1.rearrange("f o -> (f o)").partition_broadcast(P)),
                   (a2b, a2.rearrange("f o -> (f o)").partition_broadcast(P)),
                   (tb[:, :], temp.rearrange("a h b c -> (a h b c)").partition_broadcast(P)),
                   (bsr[:, :], b_slice.rearrange("(o n) -> o n", o=1))]
        wloads += [(bxc[:, c:c + 1], b_x[c * P:(c + 1) * P].rearrange("(p o) -> p o", o=1)) for c in range(NP2)]
        late = [(Wfx[:, k, :], W_fx[k * P:(k + 1) * P, :]) for k in range(2)]
        late += [(Wo[:, c, :], W_out[c * P:(c + 1) * P, :]) for c in range(NP2)]
        late += [(bfx, b_fx.rearrange("(o n) -> o n", o=1)), (bob, b_out.partition_broadcast(G))]
        for i, w in enumerate((W_q, W_k, W_v)):
            late += [(W3[k * G:(k + 1) * G, i, k * G:(k + 1) * G], w) for k in range(2)]
        LAST = NB - 1

        block = ctx.enter_context(nc.Block())

        @block.sync
        def _(sp):
            sp.wait_ge(s_clear, 1)
            for t, a in ((rowi, src), (coli, dst), (ewi, ew.bitcast(I32))):
                sp.dma_start(t[:, 0:ECOL], a[0:P * ECOL].rearrange("(p j) -> p j", p=P)).then_inc(s_edge, 16)
                sp.dma_start(t[0:EREST, ECOL:ECOL + 1],
                             a[P * ECOL:E].rearrange("(p j) -> p j", j=1)).then_inc(s_edge, 16)
            sp.wait_ge(s_clear, 3)
            for k in range(2):
                sp.dma_start(srt.rearrange("(p t) k -> p (t k)", p=P)[:, k * PITCH:(k + 1) * PITCH],
                             zero_rec).then_inc(s_zdma, 16)
            sp.dma_start(res[:, 0:LAST, :], x[0:LAST * P, :].rearrange("(b p) f -> p b f", p=P)).then_inc(s_x, 16)
            sp.dma_start(res[0:TAIL, LAST, :], x[LAST * P:N, :]).then_inc(s_x, 16)
            sp.wait_ge(s_zero, 1)
            for d, s in wloads:
                sp.dma_start(d, s).then_inc(s_w, 16)

            def store_g(b, k):
                sp.wait_ge(s_gt, b + 1)
                sp.dma_start(gtab[ds(b * P, P), :], Gt[:, k, :]).then_inc(s_gd[k], 16)

            with sp.Fori(0, NB // 2) as i:
                for k in range(2):
                    store_g(i * 2 + k, k)
            store_g(LAST, 0)

            for k in range(2):
                sp.wait_ge(s_scat[k], 16 * EC // 2)
            sp.dma_start(srec[:, :, :], srt.rearrange("(p t) k -> p t k", p=P)[:, 0:T, :]).then_inc(s_srec, 16)

            sp.wait_ge(s_nov, 1)
            nov = sp.value_load(novi[0:1, 0:1], min_val=0, max_val=OV)
            with sp.If_ne(sp.to_reg(nov), 0):
                with sp.Fori(0, nov) as t:
                    sp.wait_ge(s_oadd, t + 1)
                    sp.dma_start(orec, srt.rearrange("(p t) k -> p t k", p=P)[:, ds(t + T, 1), :]
                                 .rearrange("p o k -> p (o k)")).then_inc(s_orec, 16)
            sp.wait_ge(s_ovd, 1)
            sp.dma_start(ovs.rearrange("p b w -> p (b w)"), accf).then_inc(s_ovs, 16)
            sp.wait_ge(s_ovs, 16)

            def load_ov(b, k, start=False):
                if not start:
                    sp.wait_ge(s_ev, b - 1)
                sp.dma_start(ovr[:, k, :], ovs[:, ds(b, 1), :].rearrange("p o w -> p (o w)")).then_inc(s_ov[k], 16)

            load_ov(0, 0, True)
            load_ov(1, 1, True)
            with sp.Fori(1, NB // 2) as i:
                for k in range(2):
                    load_ov(i * 2 + k, k)
            load_ov(LAST, 0)
            sp.wait_ge(s_w3z, 1)
            for d, w in late:
                sp.dma_start(d, w).then_inc(s_w3, 16)

            def store_o(b, k, n=P):
                sp.wait_ge(s_os, b + 1)
                sp.dma_start(out[ds(b * P, n), :], ot[0:n, k, :]).then_inc(s_od[k], 16)

            with sp.Fori(0, NB // 2) as i:
                for k in range(2):
                    store_o(i * 2 + k, k)
            store_o(LAST, 0, TAIL)
            sp.wait_ge(s_od[0], 16 * (NB // 2 + 1))
            sp.wait_ge(s_od[1], 16 * (NB // 2))

        @block.gpsimd
        def _(pool):
            pool.iota(iota[:, :], pattern=[[1, P]], base=0, channel_multiplier=0,
                      allow_small_or_imprecise_dtypes=True).then_inc(s_const, 1)
            pool.iota(iotap[:, :], pattern=[[1, 1]], base=0, channel_multiplier=1,
                      allow_small_or_imprecise_dtypes=True).then_inc(s_const, 1)
            pool.iota(slotf[:, ECOL:EC], pattern=[[P, EC - ECOL]], base=P * (T + OV), channel_multiplier=1,
                      allow_small_or_imprecise_dtypes=True).then_inc(s_const, 1)
            pool.memset(ones[:, :], 1.0).then_inc(s_const, 1)
            pool.memset(onesb[:, :], 1.0).then_inc(s_const, 1)

            pool.wait_ge(s_zdma, 32)
            pool.wait_ge(s_slot, 1)

            def scatter(i, k, start=False):
                if not start:
                    pool.wait_ge(s_scat[k], i * 16 * U)
                pool.tensor_copy(ring_s[:, k, :], sloti[:, ds((i * 2 + k) * U, U)])
                pool.tensor_copy(ring_r[:, k, :, :], rec[:, ds((i * 2 + k) * U, U), :]).then_inc(s_stage, 1)
                pool.wait_ge(s_stage, i * 2 + k + 1)
                pool.sem_inc(s_tick, 1)
                for u in range(U):
                    pool.indirect_dma_start(
                        srt[:, :], bass.IndirectOffsetOnAxis(ap=ring_s[:, k, u:u + 1], axis=0),
                        ring_r[:, k, u, :], None).then_inc(s_scat[k], 16)

            for k in range(2):
                scatter(0, k, True)
            with pool.Fori(1, EC // (2 * U)) as i:
                for k in range(2):
                    scatter(i, k)

            pool.wait_ge(s_gd[0], 16 * (NB // 2 + 1))
            pool.wait_ge(s_gd[1], 16 * (NB // 2))
            pool.wait_ge(s_nov, 1)
            nov = pool.value_load(novi[0:1, 0:1], min_val=0, max_val=OV)
            with pool.If_ne(pool.to_reg(nov), 0):
                pool.wait_ge(s_clear, 4)
                pool.iota(iota_t, pattern=[[1, OV]], base=0, channel_multiplier=0,
                          allow_small_or_imprecise_dtypes=True).then_inc(s_ti, 1)
                with pool.Fori(0, nov) as t:
                    pool.wait_ge(s_oidx, t + 1)
                    pool.sem_inc(s_tick, 1)
                    pool.indirect_dma_start(
                        orow, None, gtab[:, :], bass.IndirectOffsetOnAxis(ap=oidx, axis=0)).then_inc(s_orow, 16)

            pool.wait_ge(s_ovd, 1)
            def gather(b, k, start=False):
                pool.wait_ge(s_idx, b + 1)
                for lo, hi in zip((0,) + UG, UG):
                    if not start:
                        pool.wait_ge(s_seg, b * TQ - TQ + hi)
                        pool.sem_inc(s_tick, 1)
                    for u in range(lo, hi):
                        pool.indirect_dma_start(
                            rows[:, u, :], None, gtab[:, :],
                            bass.IndirectOffsetOnAxis(ap=ring_i[:, k, u:u + 1], axis=0)).then_inc(s_row[u], 16)

            gather(0, 0, True)
            gather(1, 1)
            with pool.Fori(1, NB // 2) as i:
                for k in range(2):
                    gather(i * 2 + k, k)
            gather(LAST, 0)

        @block.vector
        def _(dve):
            step = Chain(dve, s_dve)
            v = nc.vector

            v.memset(rowi[:, ECOL:EC], NB * P)
            v.memset(coli[:, ECOL:EC], 0)
            v.memset(ewi[:, ECOL:EC], 0).then_inc(s_clear, 1)
            v.memset(zero_rec, 0).then_inc(s_clear, 1)
            v.memset(res[:, LAST, :], 0.0).then_inc(s_clear, 1)
            v.memset(Ws2[:, :], 0.0).then_inc(s_zero, 1)
            v.memset(zrow[:, :], 0.0).then_inc(s_zs, 1)
            dve.wait_ge(s_const, 5)
            v.tensor_scalar(ident[:, :], iota[:, :], iotap[:, 0:1], None, ALU.is_equal)
            v.tensor_scalar(lower, iota[:, :], iotap[:, 0:1], None, ALU.is_gt)
            v.memset(valid[:, :], 1.0)
            step(v.tensor_scalar(padf[:, :], iotap[:, :], float(TAIL), None, ALU.is_ge))
            step(v.tensor_scalar(valid[:, LAST:NB], padf[:, :], -1.0, 1.0, ALU.mult, ALU.add))

            dve.wait_ge(s_edge, 96)
            step(v.tensor_scalar(sloti, rowi, 7, None, ALU.logical_shift_right))
            step(v.tensor_scalar(tmpi, rowi, P - 1, None, ALU.bitwise_and))
            step(v.tensor_copy(hif, sloti))
            v.scalar_tensor_tensor(rec[:, :, 0], coli, 7, tmpi, ALU.logical_shift_left, ALU.bitwise_or)
            v.tensor_copy(rec[:, :, 1], ewi)
            v.memset(accf, 0.0)
            step(v.tensor_copy(cnt[:, :], valid[:, :]))
            v.tensor_copy(acc[:, LAST, F:GW], padf[:, :]).then_inc(s_dja, 1)
            with dve.Fori(0, NB // Q) as i:
                step.enter(i, 0, Q + 1)
                for q in range(Q):
                    step(v.tensor_scalar(scan, hif, iota[:, ds(i * Q + q, 1)], 0.0, ALU.is_equal, ALU.add,
                                         accum_out=part[:, q:q + 1]))
                step(v.tensor_copy(cnt[:, ds(i * Q, Q)], part[:, :]))
            step.leave(NB // Q, Q + 1)
            dve.sem_inc(s_cnt, 1)
            step(v.tensor_scalar(first[:, :], iota[:, 0:NB], float(TQ * P), None, ALU.mult))
            step(v.tensor_scalar(limit[:, :], first[:, :], float(TQ * P), None, ALU.add))
            dve.wait_ge(s_pre, 1)
            step(v.tensor_scalar(ntf[:, :], bank[0][:, 64:64 + NB], float(-TQ * P), 0.0, ALU.add, ALU.max))
            step(v.tensor_scalar(nti[:, :], ntf[:, :], float(P - 1), None, ALU.add))
            step(v.tensor_scalar(nti[:, :], nti[:, :], 7, None, ALU.logical_shift_right))
            step(v.tensor_copy(ntf[:, :], nti[:, :]))
            step(v.tensor_tensor_scan(ctf[:, :], ones[:, 0:NB], ntf[:, :], 0.0, ALU.mult, ALU.add))
            step(v.tensor_tensor(jump[:, :], ctf[:, :], ntf[:, :], ALU.subtract))
            step(v.tensor_scalar(jump[:, :], jump[:, :], float(P), float(T * P), ALU.mult, ALU.add))
            step(v.tensor_tensor(jump[:, :], jump[:, :], limit[:, :], ALU.subtract))
            step(v.tensor_tensor(base[:, :], first[:, :], bank[0][:, 0:NB], ALU.add))
            step(v.tensor_scalar(base[:, :], base[:, :], -1.0, None, ALU.add))
            v.tensor_copy(novi[:, :], ctf[0:1, NB - 1:NB]).then_inc(s_nov, 1)
            dve.wait_ge(s_nov, 1)
            with dve.Fori(0, NB) as b:
                step.enter(b, 0, 3)
                step(v.tensor_scalar(mask[:, :], hif, iota[:, ds(b, 1)], None, ALU.is_equal))
                step(v.tensor_tensor_scan(scan, onesb[:, :], mask[:, :], base[:, ds(b, 1)], ALU.mult, ALU.add))
                dve.sem_inc(s_tick, 1)
                step(v.copy_predicated(slotf, mask[:, :], scan))
            step.leave(NB, 3)
            nov = dve.value_load(novi[0:1, 0:1], min_val=0, max_val=OV)
            with dve.If_ne(dve.to_reg(nov), 0):
                with dve.Fori(0, NB) as b:
                    dve.wait_ge(s_dja, b * 3 + 1)
                    v.tensor_scalar(scan, slotf, limit[:, ds(b, 1)], jump[:, ds(b, 1)], ALU.is_ge, ALU.mult).then_inc(s_dja, 1)
                    dve.wait_ge(s_dja, b * 3 + 2)
                    v.scalar_tensor_tensor(scan, hif, iota[:, ds(b, 1)], scan, ALU.is_equal, ALU.mult).then_inc(s_dja, 1)
                    dve.wait_ge(s_dja, b * 3 + 3)
                    v.tensor_tensor(slotf, slotf, scan, ALU.add).then_inc(s_dja, 1)
                dve.wait_ge(s_dja, 3 * NB + 1)
            step(v.tensor_copy(sloti, slotf))
            step(v.tensor_scalar(tmpi, sloti, P - 1, None, ALU.bitwise_and))
            step(v.tensor_scalar(sloti, sloti, 7, None, ALU.logical_shift_right))
            step(v.tensor_copy(sf, sloti))
            step(v.scalar_tensor_tensor(slotf, tmpi, float(PITCH), sf, ALU.mult, ALU.add))
            v.tensor_copy(sloti, slotf).then_inc(s_slot, 1)

            dve.wait_ge(s_w, 16 * len(wloads))
            for k in range(2):
                step(v.tensor_tensor_reduce(xn1[:, k, :], Wg[:, k, 0:F], a2b, 1.0, 0.0, ALU.mult, ALU.add,
                                            accum_out=Wg[:, k, F:GW]))
            step(v.tensor_scalar(tb[:, :], tb[:, :], 0.1, 5.0, ALU.max, ALU.min))
            step(v.reciprocal(tb[:, :], tb[:, :]))
            dve.wait_ge(s_wxs, 1)
            tbc = tb[:, :].unsqueeze(2)
            for k in range(2):
                v.tensor_tensor(Wxs[:, k, :].rearrange("p (h g) -> p h g", g=G),
                                bank[4 + k][:, :].rearrange("p (h g) -> p h g", g=G),
                                tbc.broadcast_to([P, H, G]), ALU.mult)
            step(v.tensor_tensor(bxs[:, :].rearrange("p (h g) -> p h g", g=G),
                                 bank[3][0:1, :].rearrange("p (h g) -> p h g", g=G),
                                 bsr[:, :].unsqueeze(1).broadcast_to([1, H, G]), ALU.add))
            v.tensor_tensor(bxs[:, :].rearrange("p (h g) -> p h g", g=G),
                            bxs[:, :].rearrange("p (h g) -> p h g", g=G),
                            tb[0:1, :].unsqueeze(2).broadcast_to([1, H, G]), ALU.mult).then_inc(s_wxd, 1)

            def stats(b, view):
                return v.bn_stats(st6[:, ds(b, 1), :].rearrange("p o s -> p (o s)"), view)

            def norm_stats():
                v.tensor_tensor(mean[:, :], st6[:, :, 1], st6[:, :, 4], ALU.add)
                step(v.tensor_tensor(var[:, :], st6[:, :, 1], st6[:, :, 4], ALU.subtract))
                step(v.scalar_tensor_tensor(var[:, :], var[:, :], 0.25, var[:, :], ALU.mult, ALU.mult))
                step(v.tensor_tensor(nwt[:, :], st6[:, :, 2], st6[:, :, 5], ALU.add))
                step(v.scalar_tensor_tensor(var[:, :], nwt[:, :], 1.0 / F, var[:, :], ALU.mult, ALU.add))
                step(v.tensor_scalar(var[:, :], var[:, :], EPS, None, ALU.add))
                v.tensor_scalar(nwt[:, :], var[:, :], 1.0, None, ALU.mult).then_inc(s_var, 1)
                dve.wait_ge(s_rs0, 1)
                step(v.tensor_tensor(nwt[:, :], var[:, :], rstd[:, :], ALU.mult))
                step(v.tensor_tensor(nwt[:, :], nwt[:, :], rstd[:, :], ALU.mult))
                step(v.tensor_scalar(nwt[:, :], nwt[:, :], -0.5, 1.5, ALU.mult, ALU.add))
                step(v.tensor_tensor(rstd[:, :], rstd[:, :], nwt[:, :], ALU.mult))
                v.scalar_tensor_tensor(nmr[:, :], mean[:, :], -0.5, rstd[:, :], ALU.mult, ALU.mult).then_inc(s_rs, 1)

            dve.wait_ge(s_x, 32)
            with dve.Fori(0, NB // Q) as i:
                for q in range(Q):
                    stats(i * Q + q, res[:, ds(i * Q + q, 1), :].rearrange("p o f -> p (o f)"))
            step(v.tensor_copy(part[:, :], cnt[:, 0:Q]))
            norm_stats()

            def gate(b, k, first):
                dve.wait_ge(s_gx, b + 1)
                step(v.tensor_scalar(sm[:, k, 1:2], sm[:, k, 0:1], 1.0, None, ALU.add))
                if not first:
                    dve.wait_ge(s_gd[k], (b - k) * 8)
                step(v.reciprocal(Gt[:, k, F:GW], sm[:, k, 1:2]))
                v.tensor_scalar(Gt[:, k, 0:F], bank[3 + k][:, 0:F], Gt[:, k, F:GW], None,
                                ALU.mult).then_inc(s_gt, 1)

            gate(0, 0, True)
            gate(1, 1, True)
            with dve.Fori(1, NB // 2) as i:
                step.enter(i, 1, 4)
                for k in range(2):
                    gate(i * 2 + k, k, False)
            step.leave(NB // 2 - 1, 4)
            gate(LAST, 0, False)

            with dve.If_ne(dve.to_reg(nov), 0):
                dve.wait_ge(s_slot, 1)
                v.memset(ge, 0.0).then_inc(s_clear, 1)
                dve.wait_ge(s_ti, 1)
                dve.wait_ge(s_ctc, 1)
                v.tensor_copy(ctcol[:, :], bank[0][0:NB, 128:129]).then_inc(s_ge, 1)
                dve.wait_ge(s_ge, 1)
                v.tensor_scalar(ge[0:NB, :], iota_t[0:NB, :], ctcol[:, 0:1], None, ALU.is_ge).then_inc(s_ge, 1)
                dve.wait_ge(s_gs, 1)
                for c in range(2):
                    w = OV // 2
                    v.tensor_scalar(ge[0:1, c * w:(c + 1) * w], bank[1 + c][0:1, 0:w], float(LAST), float(GW),
                                    ALU.min, ALU.mult).then_inc(s_ge, 1)
                dve.wait_ge(s_ge, 4)
                v.tensor_copy(offi[0:1, :], ge[0:1, :]).then_inc(s_off, 1)
                dve.wait_ge(s_off, 1)
                v.memset(orow, 0.0).then_inc(s_oadd, 1)
                dve.wait_ge(s_oadd, 1)
                with dve.Fori(0, nov) as t:
                    dve.wait_ge(s_orec, t * 16 + 16)
                    v.tensor_scalar(oidx, orec[:, 0:1], 7, None, ALU.logical_shift_right).then_inc(s_oidx, 1)
                    v.tensor_scalar(olo[:, 0:1], orec[:, 0:1], P - 1, None, ALU.bitwise_and).then_inc(s_oS, 1)
                    dve.wait_ge(s_oS, t * 3 + 1)
                    v.tensor_copy(olof, olo[:, 0:1]).then_inc(s_oS, 1)
                    dve.wait_ge(s_oS, t * 3 + 2)
                    v.tensor_scalar(oS, iota[:, :], olof, oewf[:, 1:2], ALU.is_equal, ALU.mult).then_inc(s_oS, 1)
                    off = dve.value_load(offi[0:1, ds(t, 1)], min_val=0, max_val=LAST * GW)
                    dve.wait_ge(s_oseg, t + 1)
                    v.tensor_tensor(accf[:, ds(off, GW)], accf[:, ds(off, GW)], bank[0][:, 0:GW], ALU.add).then_inc(s_oadd, 1)
                    dve.wait_ge(s_oadd, t + 2)
            step(v.tensor_copy(part[:, :], iota[:, 0:Q]))
            v.tensor_copy(var[:, 0:Q], part[:, :]).then_inc(s_ovd, 1)

            dve.wait_ge(s_srec, 16)

            def decode(b, k):
                r = srec[:, ds(b * TQ, TQ), 0]
                step(v.tensor_scalar(loi[:, :], r, P - 1, None, ALU.bitwise_and))
                v.tensor_copy(lof[:, k, :], loi[:, :])
                v.tensor_scalar(ring_i[:, k, :], r, 7, None, ALU.logical_shift_right).then_inc(s_idx, 1)
                dve.wait_ge(s_idx, b + 1)

            def select(b, k, lo, hi, start=False):
                for u in range(lo, hi):
                    if not start:
                        dve.wait_ge(s_seg, b * TQ - TQ + u + 1)
                    v.tensor_scalar(S[:, u, :], iota[:, :], lof[:, k, u:u + 1], sewf[:, ds(b * TQ + u, 1), 1],
                                    ALU.is_equal, ALU.mult).then_inc(s_S, 1)

            def feat(b):
                return res[:, ds(b, 1), :].rearrange("p o f -> p (o f)")

            def take(b, k):
                dve.wait_ge(s_seg, b * TQ + TQ)
                dve.wait_ge(s_ov[k], (b - k) * 8 + 16)
                v.tensor_tensor(ag[:, :], bank[k][:, 0:GW], ovr[:, k, :], ALU.add).then_inc(s_ev, 1)
                dve.wait_ge(s_ev, b + 1)

            def gnn(b):
                step(v.reciprocal(col(RI), ag[:, F:GW]))
                step(v.scalar_tensor_tensor(neg[:, :], ag[:, 0:F], col(RI), a1b[:, :], ALU.mult, ALU.mult,
                                            accum_out=col(ZD)))
                v.scalar_tensor_tensor(col(ZA), col(ZD), -1.0, col(ZD), ALU.mult, ALU.min).then_inc(s_z1, 1)
                step(v.tensor_scalar(neg[:, :], ag[:, 0:F], col(RI), 0.0, ALU.mult, ALU.min))
                dve.wait_ge(s_l1, b * 2 + 2)
                v.scalar_tensor_tensor(col(LD), col(ZD), 0.0, col(LG), ALU.max, ALU.add).then_inc(s_l2, 1)
                dve.wait_ge(s_rel, b + 1)
                step(v.tensor_tensor(pos[:, :], pos[:, :], feat(b), ALU.add))
                dve.wait_ge(s_ex, b + 1)
                v.scalar_tensor_tensor(feat(b), neg[:, :], -1.0, pos[:, :], ALU.add, ALU.add).then_inc(s_x1, 1)
                dve.wait_ge(s_x1, b + 1)
                dve.sem_inc(s_tick, 1)
                step(v.bn_stats(bst[:, :], feat(b)))
                dve.sem_inc(s_tick, 1)
                step(v.bn_aggr(bmv[:, :], bst[:, :]))
                v.tensor_scalar(col(VA), bmv[:, 1:2], EPS, None, ALU.add).then_inc(s_var, 1)
                dve.wait_ge(s_rs0, b + 2)
                step(v.scalar_tensor_tensor(col(NW), col(VA), col(RS), col(RS), ALU.mult, ALU.mult))
                step(v.tensor_scalar(col(NW), col(NW), -0.5, 1.5, ALU.mult, ALU.add))
                step(v.tensor_tensor(col(RS), col(RS), col(NW), ALU.mult))
                v.scalar_tensor_tensor(col(NM), bmv[:, 0:1], -1.0, col(RS), ALU.mult, ALU.mult).then_inc(s_rs, 1)

            def heads(t):
                return t.rearrange("p (h g) -> p h g", g=G)

            def softmax(b, start=False):
                dve.wait_ge(s_lm, b + 1)
                step(v.tensor_reduce(hm[:, 0, :], heads(bank[4][:, :]), AX.X, ALU.max))
                v.tensor_tensor(heads(lg[:, :]), heads(bank[4][:, :]),
                                hm[:, 0, :].unsqueeze(2).broadcast_to([P, H, G]), ALU.subtract).then_inc(s_ls, 1)
                dve.wait_ge(s_le, b + 1)
                step(v.tensor_reduce(hm[:, 1, :], heads(lg[:, :]), AX.X, ALU.add))
                step(v.reciprocal(hm[:, 2, :], hm[:, 1, :]))
                if not start:
                    dve.wait_ge(s_M, b)
                v.tensor_tensor(heads(sw[:, :]), heads(lg[:, :]),
                                hm[:, 2, :].unsqueeze(2).broadcast_to([P, H, G]), ALU.mult).then_inc(s_sw, 1)

            def main(b, k, left, start=False):
                if left >= 1:
                    select(b + 1, 1 - k, AH, TQ)
                take(b, k)
                if left >= 2:
                    decode(b + 2, k)
                gnn(b)
                if left >= 2:
                    select(b + 2, k, 0, AH)
                if left == 0:
                    v.memset(W3[:, :, :], 0.0).then_inc(s_w3z, 1)
                softmax(b, start)

            decode(0, 0)
            decode(1, 1)
            select(0, 0, 0, TQ, True)
            select(1, 1, 0, AH)
            n0 = step.n
            main(0, 0, 2, True)
            main(1, 1, 2)
            per = step.n - n0
            with dve.Fori(1, NB // 2 - 1) as i:
                step.enter(i, 1, per)
                for k in range(2):
                    main(i * 2 + k, k, 2)
            step.leave(NB // 2 - 2, per)
            main(NB - 3, 0, 2)
            main(NB - 2, 1, 1)
            main(NB - 1, 0, 0)

            dve.wait_ge(s_M, NB)
            for t in (tokd, qd, vd, ad):
                v.memset(t[:, :, :], 0.0)
            step(v.tensor_scalar(nrm[:, 0, :], bank[5][:, 0:NP2], 1e-5, None, ALU.add))
            step(v.reciprocal(nrm[:, 1, :], nrm[:, 0, :]))
            step(v.tensor_tensor(nrm[:, 2, :], bank[5][:, 0:NP2], nrm[:, 1, :], ALU.mult))
            for c in range(NP2):
                m = v.tensor_scalar(Mn[:, c, :], bank[2 + c // 2][:, (c % 2) * F:(c % 2 + 1) * F], nrm[:, 1, c:c + 1], None,
                                    ALU.mult)
            m.then_inc(s_mic, 1)
            mid = [0]

            def waitmid():
                mid[0] += 1
                dve.wait_ge(s_mid, mid[0])

            waitmid()
            v.tensor_copy(MnT[:, 0, :], bank[4][:, :])
            v.tensor_copy(MnT[:, 1, :], bank[5][:, :])
            v.tensor_copy(nbT, bank[6][0:1, :]).then_inc(s_mic, 1)

            def halves(dst, psum, last=None):
                w = psum.rearrange("p (c n) -> p c n", n=P)
                v.tensor_copy(dst[0:G, :, 0:G], w[0:G, :, 0:G])
                return v.tensor_copy(dst[G:P, :, G:P], w[G:P, :, G:P])

            waitmid()
            halves(tokd, bank[7][:, :])
            w7 = bank[7][:, :].rearrange("p (c n) -> p c n", n=P)
            v.tensor_copy(tokc[0:G, :, :], w7[0:G, :, 0:G])
            v.tensor_copy(tokc[G:P, :, :], w7[G:P, :, G:P]).then_inc(s_mic, 1)
            waitmid()
            halves(qd, bank[4][:, :])
            v.tensor_copy(kc[:, :, :], bank[5][:, 0:NP2 * G].rearrange("p (c n) -> p c n", n=G))
            halves(vd, bank[6][:, :]).then_inc(s_mic, 1)
            waitmid()
            sc = bank[7][:, 0:NP2 * G].rearrange("p (c n) -> p c n", n=G)
            step(v.tensor_reduce(nrm[:, 0, :], sc, AX.X, ALU.max))
            v.tensor_tensor(al[:, :, :], sc, nrm[:, 0, :].unsqueeze(2).broadcast_to([P, NP2, G]),
                            ALU.subtract).then_inc(s_mic, 1)
            dve.wait_ge(s_mia, 1)
            step(v.tensor_reduce(nrm[:, 1, :], al[:, :, :], AX.X, ALU.add))
            step(v.reciprocal(nrm[:, 2, :], nrm[:, 1, :]))
            for lo in (0, G):
                m = v.tensor_tensor(ad[lo:lo + G, :, lo:lo + G], al[lo:lo + G, :, :],
                                    nrm[lo:lo + G, 2, :].unsqueeze(2).broadcast_to([G, NP2, G]), ALU.mult)
            m.then_inc(s_mic, 1)
            waitmid()
            v.tensor_copy(aT[:, :, :], bank[4][:, :].rearrange("p (c n) -> p c n", n=P)).then_inc(s_mic, 1)
            waitmid()
            v.tensor_copy(oT[:, :, :], bank[5][:, :].rearrange("p (c n) -> p c n", n=P)).then_inc(s_mic, 1)
            waitmid()
            for c in range(NP2):
                m = v.tensor_copy(Pm[:, c, :], bank[6 + c // 2][:, (c % 2) * F:(c % 2 + 1) * F])
            step(m)
            v.tensor_tensor(Pm[0:G, 0, :], Pm[0:G, 0, :], bob, ALU.add).then_inc(s_mic, 1)

            def result(b, k, first):
                dve.wait_ge(s_o, b + 1)
                if not first:
                    dve.wait_ge(s_od[k], (b - k) * 8)
                v.tensor_tensor(ot[:, k, :], bank[4 + k][:, 0:F], feat(b), ALU.add).then_inc(s_os, 1)

            result(0, 0, True)
            result(1, 1, True)
            with dve.Fori(1, NB // 2) as i:
                for k in range(2):
                    result(i * 2 + k, k, False)
            result(LAST, 0, False)

        @block.scalar
        def _(act):
            a = nc.scalar
            a.preload_act_table_set("natural_log_exp_and_others")
            step = Chain(act, s_act)

            for k in range(2):
                act.wait_ge(s_wxt, k + 1)
                a.copy(WxT[:, :, k * P:(k + 1) * P], bank[6 + k][:, :].rearrange("p (c n) -> p c n", n=P)).then_inc(s_wxc, 1)

            def guess(n, d, t, v):
                act.wait_ge(s_var, n)
                step(a.activation(t, v, ACT.Ln))
                a.activation(d, t, ACT.Exp, scale=-0.5).then_inc(s_rs0, 1)

            guess(1, rstd[:, :], lnv[:, :], nwt[:, :])
            act.wait_ge(s_rs, 1)

            def stage1(b, k, first):
                if not first:
                    act.wait_ge(s_xt, b - 1)
                a.activation(xn1[:, k, :], res[:, ds(b, 1), :].rearrange("p o f -> p (o f)"), ACT.Identity,
                             bias=nmr[:, ds(b, 1)], scale=rstd[:, ds(b, 1)]).then_inc(s_xn, 1)
                act.wait_ge(s_xt, b + 1)
                if not first:
                    act.wait_ge(s_gm, b - 1)
                a.copy(xT1[:, k, :], bank[6 + k][:, 0:F]).then_inc(s_xc, 1)
                act.wait_ge(s_gm, b + 1)
                if not first:
                    act.wait_ge(s_gt, b - 1)
                a.activation(sm[:, k, 0:1], bank[3 + k][:, F:GW], ACT.Exp, scale=-1.0).then_inc(s_gx, 1)

            stage1(0, 0, True)
            stage1(1, 1, True)
            with act.Fori(1, NB // 2) as i:
                for k in range(2):
                    stage1(i * 2 + k, k, False)
            stage1(LAST, 0, False)

            def main(b, start=False):
                act.wait_ge(s_z1, b + 1)
                a.activation(col(EX), col(ZA), ACT.Exp).then_inc(s_l1, 1)
                act.wait_ge(s_l1, b * 2 + 1)
                a.activation(col(LG), col(EX), ACT.Ln, bias=1.0).then_inc(s_l1, 1)
                if not start:
                    act.wait_ge(s_x1, b)
                a.activation(pos[:, :], ag[:, 0:F], ACT.Relu, scale=col(RI)).then_inc(s_rel, 1)
                act.wait_ge(s_l2, b + 1)
                a.activation(neg[:, :], neg[:, :], ACT.Exp, scale=col(LD)).then_inc(s_ex, 1)
                step.n = 1
                step.loop = b
                guess(b + 2, col(RS), col(LV), col(VA))
                act.wait_ge(s_rs, b + 2)
                if not start:
                    act.wait_ge(s_M, b)
                a.activation(xn[:, :], res[:, ds(b, 1), :].rearrange("p o f -> p (o f)"), ACT.Identity,
                             bias=col(NM), scale=col(RS)).then_inc(s_xn, 1)
                if not start:
                    keep(b - 1)
                act.wait_ge(s_xt, b + NB + 1)
                if not start:
                    act.wait_ge(s_lm, b)
                a.copy(xT[:, :], bank[6][:, 0:F]).then_inc(s_xc, 1)
                act.wait_ge(s_ls, b + 1)
                a.activation(lg[:, :], lg[:, :], ACT.Exp).then_inc(s_le, 1)

            def keep(b):
                act.wait_ge(s_wt, b + 1)
                a.copy(swt[:, :, ds(b * P, P)], bank[7][:, :].rearrange("p (c n) -> p c n", n=P)).then_inc(s_wc, 1)

            act.wait_ge(s_ovs, 16)
            main(0, True)
            with act.Fori(1, NB) as b:
                main(b)
            keep(LAST)

            act.wait_ge(s_mic, 5)
            a.activation(al[:, :, :], al[:, :, :], ACT.Exp, scale=SCALE).then_inc(s_mia, 1)

            act.wait_ge(s_mic, 9)
            def load(b, k, first):
                if not first:
                    act.wait_ge(s_o, b - 1)
                a.copy(stg[:, k, :].rearrange("p (c n) -> p c n", n=P), swt[:, :, ds(b * P, P)]).then_inc(s_wl, 1)

            load(0, 0, True)
            load(1, 1, True)
            with act.Fori(1, NB // 2) as i:
                for k in range(2):
                    load(i * 2 + k, k, False)
            load(LAST, 0, False)

        @block.tensor
        def _(pe):
            def mm(o, l, r, start=True, stop=True):
                return nc.tensor.matmul(o, l, r, start=start, stop=stop, skip_group_check=True)

            pe.wait_ge(s_w, 16 * len(wloads))
            pe.wait_ge(s_dve, 2)
            for k in range(2):
                for c in range(NP2):
                    t = nc.tensor.transpose(bank[6 + k][:, c * P:(c + 1) * P], Wxr[:, k, c // 2, (c % 2) * P:(c % 2 + 1) * P], ident[:, :])
                t.then_inc(s_wxt, 1)
            pe.wait_ge(s_wxc, 2)
            for c in range(NP2):
                for k in range(2):
                    mm(bank[4 + k][:, c * P:(c + 1) * P], WxT[:, c, k * P:(k + 1) * P], Ws2[:, :])
                m = mm(bank[3][0:1, c * P:(c + 1) * P], bxc[:, c:c + 1], Ws2[:, :])
            m.then_inc(s_wxs, 1)

            pe.wait_ge(s_cnt, 1)
            mm(bank[0][:, 0:NB], lower, cnt[:, :])
            mm(bank[0][:, 64:64 + NB], ones[:, :], cnt[:, :]).then_inc(s_pre, 1)

            pe.wait_ge(s_wxd, 1)
            def transposes(n, src, ps):
                pe.wait_ge(s_xn, n + 1)
                for c in range(2):
                    t = nc.tensor.transpose(ps[:, c * P:(c + 1) * P], src[:, c * P:(c + 1) * P], ident[:, :])
                t.then_inc(s_xt, 1)

            def support(b, k, first):
                if not first:
                    pe.wait_ge(s_xc, b - 1)
                transposes(b, xn1[:, k, :], bank[6 + k])
                pe.wait_ge(s_xc, b + 1)
                if not first:
                    pe.wait_ge(s_gt, b - 1)
                mm(bank[3 + k][:, 0:GW], xT1[:, k, 0:P], Wg[:, 0, :], True, False)
                mm(bank[3 + k][:, 0:GW], xT1[:, k, P:F], Wg[:, 1, :], False, True).then_inc(s_gm, 1)

            support(0, 0, True)
            support(1, 1, True)
            with pe.Fori(1, NB // 2) as i:
                for k in range(2):
                    support(i * 2 + k, k, False)
            support(LAST, 0, False)

            pe.wait_ge(s_nov, 1)
            nov = pe.value_load(novi[0:1, 0:1], min_val=0, max_val=OV)
            with pe.If_ne(pe.to_reg(nov), 0):
                mm(bank[0][0:NB, 128:129], ctf[0:1, :], ones[0:1, 0:1]).then_inc(s_ctc, 1)
                pe.wait_ge(s_ge, 2)
                for c in range(2):
                    w = OV // 2
                    m = mm(bank[1 + c][0:1, 0:w], ones[0:NB, 0:1], ge[0:NB, c * w:(c + 1) * w])
                m.then_inc(s_gs, 1)
                pe.wait_ge(s_off, 1)
                with pe.Fori(0, nov) as t:
                    pe.wait_ge(s_orow, t * 16 + 16)
                    pe.wait_ge(s_oS, t * 3 + 3)
                    pe.wait_ge(s_oadd, t + 1)
                    mm(bank[0][:, 0:GW], oS, orow).then_inc(s_oseg, 1)

            pe.wait_ge(s_zs, 1)
            pe.wait_ge(s_wxd, 1)
            pe.wait_ge(s_ovd, 1)
            for c in (2, 3, 5):
                m = mm(bank[c][:, :], zrow[0:1, 0:P], bxs[:, :], True, False)
            m.then_inc(s_mz, 1)

            def segment(b, k, lo, hi, start=False):
                for u in range(lo, hi):
                    pe.wait_ge(s_row[u], b * 16 + 16)
                    pe.wait_ge(s_S, b * TQ + u + 1)
                    if u == 0 and not start:
                        pe.wait_ge(s_ev, b - 1)
                    mm(bank[k][:, 0:GW], S[:, u, :], rows[:, u, :], u == 0, u == TQ - 1).then_inc(s_seg, 1)

            def logits(b, start=False):
                if not start:
                    pe.wait_ge(s_ls, b)
                pe.wait_ge(s_xc, b + NB + 1)
                mm(bank[4][:, :], ones[0:1, :], bxs[:, :], True, False)
                mm(bank[4][:, :], xT[:, 0:P], Wxs[:, 0, :], False, False)
                mm(bank[4][:, :], xT[:, P:F], Wxs[:, 1, :], False, True).then_inc(s_lm, 1)

            def sums(b, start=False):
                pe.wait_ge(s_sw, b + 1)
                if not start:
                    pe.wait_ge(s_wc, b)
                for c in range(NP2):
                    t = nc.tensor.transpose(bank[7][:, c * P:(c + 1) * P], sw[:, c * P:(c + 1) * P], ident[:, :])
                t.then_inc(s_wt, 1)
                for c in range(NP2):
                    w = sw[:, c * P:(c + 1) * P]
                    mm(bank[2 + c // 2][:, (c % 2) * F:(c % 2 + 1) * F], w, xn[:, :], False, False)
                    m = mm(bank[5][:, c:c + 1], w, valid[:, ds(b, 1)], False, False)
                m.then_inc(s_M, 1)

            def main(b, k, left, start=False, second=False):
                if left:
                    segment(b + 1, 1 - k, 0, 4, start)
                if not start:
                    sums(b - 1, second)
                if left:
                    segment(b + 1, 1 - k, 4, 10)
                transposes(b + NB, xn[:, :], bank[6][:, 0:F])
                if left:
                    segment(b + 1, 1 - k, 10, 12)
                logits(b, start)
                if left:
                    segment(b + 1, 1 - k, 12, TQ)

            segment(0, 0, 0, TQ, True)
            main(0, 0, True, True)
            main(1, 1, True, False, True)
            with pe.Fori(1, NB // 2) as i:
                for k in range(2):
                    main(i * 2 + k, k, True)
            main(LAST, 0, False)
            sums(LAST)

            mic = [0]

            def waitmic(n=1):
                mic[0] += n
                pe.wait_ge(s_mic, mic[0])

            pe.wait_ge(s_wc, NB)
            pe.wait_ge(s_w3, 16 * len(late))
            waitmic()
            for c in range(NP2):
                for f in range(2):
                    nc.tensor.transpose(bank[4 + f][:, c * P:(c + 1) * P], Mn[:, c, f * P:(f + 1) * P], ident[:, :])
                t = nc.tensor.transpose(bank[6][0:1, c * P:(c + 1) * P], nrm[:, 2, c:c + 1], ident[:, :])
            t.then_inc(s_mid, 1)
            waitmic()
            for c in range(NP2):
                o = bank[7][:, c * P:(c + 1) * P]
                cs = slice(c * P, (c + 1) * P)
                mm(o, Wfx[:, 0, cs], MnT[:, 0, cs], True, False)
                mm(o, Wfx[:, 1, cs], MnT[:, 1, cs], False, False)
                m = mm(o, bfx[:, cs], nbT[:, cs], False, True)
            m.then_inc(s_mid, 1)
            waitmic()
            for c in range(NP2):
                mm(bank[4][:, c * P:(c + 1) * P], W3[:, 0, :], tokd[:, c, :])
                mm(bank[5][:, c * G:(c + 1) * G], W3[:, 1, :], tokc[:, c, :])
                m = mm(bank[6][:, c * P:(c + 1) * P], tokd[:, c, :], W3[:, 2, :])
            m.then_inc(s_mid, 1)
            waitmic()
            for c in range(NP2):
                m = mm(bank[7][:, c * G:(c + 1) * G], qd[:, c, :], kc[:, c, :])
            m.then_inc(s_mid, 1)
            waitmic(2)
            for c in range(NP2):
                t = nc.tensor.transpose(bank[4][:, c * P:(c + 1) * P], ad[:, c, :], ident[:, :])
            t.then_inc(s_mid, 1)
            waitmic()
            for c in range(NP2):
                m = mm(bank[5][:, c * P:(c + 1) * P], vd[:, c, :], aT[:, c, :])
            m.then_inc(s_mid, 1)
            waitmic()
            for c in range(NP2):
                m = mm(bank[6 + c // 2][:, (c % 2) * F:(c % 2 + 1) * F], oT[:, c, :], Wo[:, c, :])
            m.then_inc(s_mid, 1)
            waitmic()

            def product(b, k, first):
                pe.wait_ge(s_wl, b + 1)
                if not first:
                    pe.wait_ge(s_os, b - 1)
                for c in range(NP2):
                    m = mm(bank[4 + k][:, 0:F], stg[:, k, c * P:(c + 1) * P], Pm[:, c, :], c == 0, c == NP2 - 1)
                m.then_inc(s_o, 1)

            product(0, 0, True)
            product(1, 1, True)
            with pe.Fori(1, NB // 2) as i:
                for k in range(2):
                    product(i * 2 + k, k, False)
            product(LAST, 0, False)


_INS = ['x', 'src', 'dst', 'edge_weight', 'L0_gnn_W', 'L0_gnn_a1', 'L0_gnn_a2', 'L0_ffn_W_fx', 'L0_ffn_b_fx',
        'L0_ffn_W_x', 'L0_ffn_b_x', 'L0_ffn_W_slice', 'L0_ffn_b_slice', 'L0_ffn_W_q', 'L0_ffn_W_k', 'L0_ffn_W_v',
        'L0_ffn_W_out', 'L0_ffn_b_out', 'L0_ffn_temperature']


def kernel(**inputs):
    import numpy as _np
    import concourse.bacc as _bacc
    from concourse import mybir as _mybir
    from concourse.bass_utils import run_bass_kernel_spmd as _run

    nc = _bacc.Bacc("TRN2", target_bir_lowering=False, num_devices=1)
    arrays, args = {}, []
    for name in _INS:
        a = _np.ascontiguousarray(inputs[name])
        arrays[f"in_{name}_dram"] = a
        args.append(nc.dram_tensor(f"in_{name}_dram", a.shape, _mybir.dt.from_np(a.dtype), kind="ExternalInput").ap())
    out = nc.dram_tensor("out_0_dram", (N, F), F32, kind="ExternalOutput").ap()
    gtab = nc.dram_tensor("gated_rows_dram", (NB * P, GW), F32, kind="Internal").ap()
    srt = nc.dram_tensor("sorted_edges_dram", (P * PITCH, 2), I32, kind="Internal").ap()
    ovs = nc.dram_tensor("overflow_sums_dram", (P, NB, GW), F32, kind="Internal").ap()
    build(nc, *args, out, gtab, srt, ovs)
    r = _run(nc, [arrays], core_ids=[0])
    return r.results[0]["out_0_dram"]
```

```python
import numpy as np
from contextlib import ExitStack

import concourse.bass as bass
from concourse import mybir

F32 = mybir.dt.float32
BF16 = mybir.dt.bfloat16
I32 = mybir.dt.int32
U8 = mybir.dt.uint8
ALU = mybir.AluOpType
ACT = mybir.ActivationFunctionType
AX = mybir.AxisListType

P = 128
N = 6250
F = 256
E = 106250
NB = -(-N // P)
TAIL = N - (NB - 1) * P
ECOL = E // P
EREST = E - ECOL * P
EC = -(-(ECOL + 1) // 32) * 32
TQ = 18
TS = TQ - 1
T = NB * TQ
OV = -(-(E // P + NB) // 2) * 2
PB = TQ * P + P
LL = NB * PB + OV * P + (EC - ECOL) * P
GC = 32
HC = GC // 2
RUN = 80
NG = EC // GC
HS = HC + 1
VB = 2 * NB
G0 = 2
assert NG % 2 == 0 and (NG - G0) * 2 == NB - 1
UG = (5, 10, 15, TQ)
BF = 5
AH = 9
H = 8
G = 64
D = 64
HG = H * G
NP2 = H // 2
GW = F + 1
U = 8
Q = 7
assert NB % Q == 0
EPS = 1e-5
SCALE = float(D) ** -0.5
ds = bass.ds


class Chain:

    def __init__(self, eng, sem):
        self.eng, self.sem, self.n, self.loop, self.per = eng, sem, 0, 0, 0

    def __call__(self, ins):
        ins.then_inc(self.sem, 1)
        self.n += 1
        self.eng.wait_ge(self.sem, self.loop + self.n)
        return self

    def enter(self, i, first, per):
        self.loop = (i - first) * per

    def leave(self, count, per):
        self.loop = 0
        self.n += (count - 1) * per


def build(nc, x, src, dst, ew, W, a1, a2, W_fx, b_fx, W_x, b_x, W_slice, b_slice, W_q, W_k, W_v,
          W_out, b_out, temp, out, gtab, srt, ovs):
    with ExitStack() as ctx:
        def sb(name, shape, dt=F32):
            return ctx.enter_context(nc.sbuf_tensor(name, shape, dt))

        def sem(name):
            return ctx.enter_context(nc.semaphore(name))

        bank = [ctx.enter_context(nc.psum_tensor(f"bank{i}", [P, 512], F32)) for i in range(8)]

        res = sb("res", [P, NB, F])
        big = sb("big", [P, 4 * NB * P])
        swt = big[:, :].rearrange("p (c n) -> p c n", c=4)
        accf = big[:, 0:NB * GW]
        srec = sb("srec", [P, 2, T])
        RW = max(TQ * GW, 4736)
        SW = max(TQ * P, 2308)
        rows_t = sb("rows", [P, RW])
        rows = rows_t[:, 0:TQ * GW].rearrange("p (u w) -> p u w", w=GW)
        S_t = sb("S", [P, SW])
        S = S_t[:, 0:TQ * P].rearrange("p (u r) -> p u r", r=P)

        class Carve:

            def __init__(self, t, at, end):
                self.t, self.at, self.end = t, at, end

            def __call__(self, n, dt=F32):
                v = self.t[:, self.at:self.at + n]
                self.at += n
                assert self.at <= self.end
                return v if dt == F32 else v.bitcast(dt)

        carve = Carve(big, NB * GW, 4 * NB * P)
        rowi = carve(EC, I32)
        coli = carve(EC, I32)
        ewf = carve(EC)
        packf = carve(EC)
        hif = carve(EC)
        hib = carve(EC // 2, BF16)
        rankf = carve(EC)
        slotf = carve(EC)
        scan = carve(EC)
        sloti = carve(EC, I32)
        tmpi = carve(EC, I32)
        zeros = carve(LL // P)
        cnt, ntf, ctf, base = carve(NB), carve(NB), carve(NB), carve(NB)
        nti = carve(NB, I32)
        first = carve(NB)
        limit = carve(NB)
        jump = carve(NB)
        st6 = carve(6 * NB).rearrange("p (b s) -> p b s", s=6)
        mean = carve(NB)
        var, lnv, rstd, nmr, nwt = carve(NB), carve(NB), carve(NB), carve(NB), carve(NB)
        carve = Carve(rows_t, 0, RW)
        mask = carve(EC // 4, U8)
        onesb = carve(EC // 2, BF16)
        lower = carve(P)
        lowerb = carve(P // 2, BF16)
        iotab = carve(P // 2, BF16)
        iota1 = carve(P)
        carve = Carve(big, 0, NB * GW)
        hot_s = [carve(HC * RUN).rearrange("p (j s) -> p j s", s=RUN) for k in range(2)]
        hot_v = [carve(HC * VB).rearrange("p (j v b) -> p j v b", v=2, b=NB) for k in range(2)]
        def halved(t, j=HS):
            return t.rearrange("p (b h j) -> p b h j", h=2, j=j)

        flags = [carve(NB * HS, BF16) for k in range(2)]
        flags4 = [halved(t) for t in flags]
        reset = carve(NB * HS, BF16)
        run = carve(NB * HS, BF16)
        run4 = halved(run)
        buckets = halved(carve(NB * HC, BF16), HC)
        prod = carve(NB * HC, BF16)
        cntp = [carve(2 * NB, BF16).rearrange("p (h v b) -> p h v b", h=2, v=2) for k in range(2)]
        runs = [carve(2 * RUN)[0:VB, :] for k in range(2)]
        neededf = carve(NB)[0:1, :]
        sumf = carve(NB)[0:1, :]
        firstc = carve(1)
        over = carve(1)
        oneb = carve(1, BF16)
        carve = Carve(rows_t, 0, RW)
        offi = carve(OV, I32)
        iota_t = carve(OV)
        ge = carve(OV)
        orec = carve(2)
        oreci = carve(1, I32)
        oidx = carve(1, I32)
        olo = carve(2, I32)
        olof = carve(1)
        orow = carve(GW)
        oS = carve(P)
        carve = Carve(S_t, 0, SW)
        Wg = carve(2 * GW).rearrange("p (k w) -> p k w", k=2)
        Gt = carve(2 * GW).rearrange("p (k w) -> p k w", k=2)
        a2b = carve(F)
        xn1 = carve(2 * F).rearrange("p (k f) -> p k f", k=2)
        xT1 = carve(2 * F).rearrange("p (k f) -> p k f", k=2)
        carve = Carve(rows_t, 0, RW)
        Wfx = carve(2 * HG).rearrange("p (k n) -> p k n", k=2)
        Wo = carve(NP2 * F).rearrange("p (c f) -> p c f", f=F)
        Pm = carve(NP2 * F).rearrange("p (c f) -> p c f", f=F)
        bfx = carve(HG)[0:1, :]
        nbT = carve(HG)[0:1, :]
        bob = carve(F)[0:G, :]
        W3 = carve(3 * P).rearrange("p (i n) -> p i n", n=P)
        carve = Carve(S_t, 0, SW)
        stg = carve(2 * HG).rearrange("p (k n) -> p k n", k=2)
        ot = carve(2 * F).rearrange("p (k f) -> p k f", k=2)
        iota = sb("iota", [P, P])
        iotap = sb("iotap", [P, 1])
        ident = sb("ident", [P, P])
        ones = sb("ones", [P, P])
        valid = sb("valid", [P, NB])
        padf = sb("padf", [P, 1])
        zcol = sb("zcol", [P, 1])
        a1b = sb("a1b", [P, F])
        Wxs = sb("Wxs", [P, 2, HG])
        bxs = sb("bxs", [1, HG])
        zrow = sb("zrow", [1, P])
        Ws2 = sb("Ws2", [P, P])
        tb = sb("tb", [P, H])
        bsr = sb("bsr", [1, G])
        bxc = sb("bxc", [P, NP2])
        Wxr = srec[:, :, :].rearrange("p t k -> p (t k)")[:, 0:1024].rearrange("p (k m f) -> p k m f", k=2, m=2)
        WxT = rows_t[:, 2048:2048 + 1024].rearrange("p (c f) -> p c f", f=F)
        novi = sb("novi", [1, 1], I32)
        slowi = sb("slowi", [1, 1], I32)
        neededi = sb("neededi", [1, 2, NB], I32)
        idx = sb("idx", [VB, 2, 2], I32)
        ctcol = sb("ctcol", [NB, 1])
        part = sb("part", [P, Q])
        sm = sb("sm", [P, 2, 4])
        hm = sb("hm", [P, 3, H])
        RI, ZD, ZA, EX, LG, LD, VA, LV, RS, NW, NM = range(11)
        bc = sb("bc", [P, 11])
        bst = sb("bst", [P, 6])
        bmv = sb("bmv", [P, 2])

        def col(n):
            return bc[:, n:n + 1]

        ring_s = sb("ring_s", [P, 2, U], I32)
        ring_r = sb("ring_r", [P, 2, U])
        ring_i = sb("ring_i", [P, 2, TQ], I32)
        loi = sb("loi", [P, TQ], I32)
        pki = sb("pki", [P, TQ], I32)
        lof = sb("lof", [P, 2, TQ])
        ovr = sb("ovr", [P, 2, GW])
        ag = sb("ag", [P, GW])
        xn = sb("xn", [P, F])
        xT = sb("xT", [P, F])
        pos = sb("pos", [P, F])
        neg = sb("neg", [P, F])
        lg = sb("lg", [P, HG])
        sw = sb("sw", [P, HG])

        def pairs(t, n=P):
            return t.rearrange("p (c n) -> p c n", n=n)

        MnT = S_t[:, 0:2 * HG].rearrange("p (k n) -> p k n", k=2)
        Mn = S_t[:, 2 * HG:4 * HG].rearrange("p (c f) -> p c f", f=F)
        tokc = pairs(S_t[:, 4 * HG:4 * HG + F], G)
        srf = srec[:, :, :].rearrange("p k t -> p (k t)")
        tokd = pairs(srf[:, 0:HG])
        qd = pairs(srf[:, HG:2 * HG])
        vd = pairs(srf[:, 2 * HG:3 * HG])
        kc = pairs(pos[:, :], G)
        ad = pairs(Wxs[:, 0, :])
        aT = pairs(Wxs[:, 1, :])
        oT = pairs(lg[:, :])
        al = pairs(sw[:, 0:F], G)
        nrm = sb("nrm", [P, 3, NP2])

        s_const = sem("s_const")
        s_tick = sem("s_tick")
        s_clear = sem("s_clear")
        s_zero = sem("s_zero")
        s_edge = sem("s_edge")
        s_zdma = sem("s_zdma")
        s_x = sem("s_x")
        s_w = sem("s_w")
        s_dve = sem("s_dve")
        s_act = sem("s_act")
        s_cnt = sem("s_cnt")
        s_pre = sem("s_pre")
        s_ctc = sem("s_ctc")
        s_slot = sem("s_slot")
        s_stage = sem("s_stage")
        s_scat = [sem(f"s_scat{k}") for k in range(2)]
        s_pack = sem("s_pack")
        s_flag = sem("s_flag")
        s_base = sem("s_base")
        s_bs = sem("s_bs")
        s_cp = sem("s_cp")
        s_tot = sem("s_tot")
        s_idx0 = sem("s_idx0")
        s_g1 = sem("s_g1")
        s_gr = sem("s_gr")
        s_prod = sem("s_prod")
        s_hs = sem("s_hs")
        s_hv = sem("s_hv")
        s_put = sem("s_put")
        s_out = sem("s_out")
        s_run = sem("s_run")
        s_long = sem("s_long")
        s_longt = sem("s_longt")
        s_need = sem("s_need")
        s_slow = sem("s_slow")
        s_gen = sem("s_gen")
        s_srec0 = sem("s_srec0")
        s_srec1 = sem("s_srec1")
        s_free = sem("s_free")
        s_ti = sem("s_ti")
        s_ge = sem("s_ge")
        s_gs = sem("s_gs")
        s_nov = sem("s_nov")
        s_off = sem("s_off")
        s_orec = sem("s_orec")
        s_oidx = sem("s_oidx")
        s_orow = sem("s_orow")
        s_oS = sem("s_oS")
        s_oseg = sem("s_oseg")
        s_oadd = sem("s_oadd")
        s_ovd = sem("s_ovd")
        s_ovs = sem("s_ovs")
        s_ov = [sem(f"s_ov{k}") for k in range(2)]
        s_ev = sem("s_ev")
        s_wxt = sem("s_wxt")
        s_wxc = sem("s_wxc")
        s_wxs = sem("s_wxs")
        s_wxd = sem("s_wxd")
        s_var = sem("s_var")
        s_rs0 = sem("s_rs0")
        s_rs = sem("s_rs")
        s_xn = sem("s_xn")
        s_xt = sem("s_xt")
        s_xc = sem("s_xc")
        s_gm = sem("s_gm")
        s_gx = sem("s_gx")
        s_gt = sem("s_gt")
        s_gd = [sem(f"s_gd{k}") for k in range(2)]
        s_idx = sem("s_idx")
        s_row = [sem(f"s_row{u}") for u in range(TQ)]
        s_S = sem("s_S")
        s_seg = sem("s_seg")
        s_rel = sem("s_rel")
        s_ex = sem("s_ex")
        s_x1 = sem("s_x1")
        s_w3z = sem("s_w3z")
        s_w3 = sem("s_w3")
        s_z1 = sem("s_z1")
        s_l1 = sem("s_l1")
        s_l2 = sem("s_l2")
        s_zs = sem("s_zs")
        s_lm = sem("s_lm")
        s_ls = sem("s_ls")
        s_le = sem("s_le")
        s_sw = sem("s_sw")
        s_wt = sem("s_wt")
        s_wc = sem("s_wc")
        s_M = sem("s_M")
        s_mid = sem("s_mid")
        s_mic = sem("s_mic")
        s_mn = sem("s_mn")
        s_ma = sem("s_ma")
        s_mia = sem("s_mia")
        s_wl = sem("s_wl")
        s_o = sem("s_o")
        s_os = sem("s_os")
        s_od = [sem(f"s_od{k}") for k in range(2)]

        wloads = []
        for k in range(2):
            wloads += [(Wg[:, k, 0:F], W[k * P:(k + 1) * P, :]),
                       (Wxr[:, k, :, :], W_x[k * P:(k + 1) * P, :].rearrange("p (m f) -> p m f", m=2)),
                       (Ws2[k * G:(k + 1) * G, k * G:(k + 1) * G], W_slice)]
        wloads += [(a1b[:, :], a1.rearrange("f o -> (f o)").partition_broadcast(P)),
                   (a2b, a2.rearrange("f o -> (f o)").partition_broadcast(P)),
                   (tb[:, :], temp.rearrange("a h b c -> (a h b c)").partition_broadcast(P)),
                   (bsr[:, :], b_slice.rearrange("(o n) -> o n", o=1))]
        wloads += [(bxc[:, c:c + 1], b_x[c * P:(c + 1) * P].rearrange("(p o) -> p o", o=1)) for c in range(NP2)]
        late = [(Wfx[:, k, :], W_fx[k * P:(k + 1) * P, :]) for k in range(2)]
        late += [(Wo[:, c, :], W_out[c * P:(c + 1) * P, :]) for c in range(NP2)]
        late += [(bfx, b_fx.rearrange("(o n) -> o n", o=1)), (bob, b_out.partition_broadcast(G))]
        for i, w in enumerate((W_q, W_k, W_v)):
            late += [(W3[k * G:(k + 1) * G, i, k * G:(k + 1) * G], w) for k in range(2)]
        LAST = NB - 1

        block = ctx.enter_context(nc.Block())

        @block.sync
        def _(sp):
            sp.wait_ge(s_clear, 1)
            for t, a in ((rowi, src), (coli, dst), (ewf, ew)):
                sp.dma_start(t[:, 0:ECOL], a[0:P * ECOL].rearrange("(p j) -> p j", p=P)).then_inc(s_edge, 16)
                sp.dma_start(t[0:EREST, ECOL:ECOL + 1],
                             a[P * ECOL:E].rearrange("(p j) -> p j", j=1)).then_inc(s_edge, 16)
            sp.wait_ge(s_clear, 3)
            sp.wait_ge(s_zero, 1)
            for k in range(2):
                sp.dma_start(srt[k * LL:k * LL + NB * PB, :].rearrange("(p t) o -> p (t o)", p=P),
                             zeros[:, 0:NB * PB // P]).then_inc(s_zdma, 16)
            for d, s in wloads:
                sp.dma_start(d, s).then_inc(s_w, 16)
            sp.dma_start(res[:, 0:LAST, :], x[0:LAST * P, :].rearrange("(b p) f -> p b f", p=P)).then_inc(s_x, 16)
            sp.dma_start(res[0:TAIL, LAST, :], x[LAST * P:N, :]).then_inc(s_x, 16)

            def store_g(b, k):
                sp.wait_ge(s_gt, b + 1)
                sp.dma_start(gtab[ds(b * P, P), :], Gt[:, k, :]).then_inc(s_gd[k], 16)

            with sp.Fori(0, NB // 2) as i:
                for k in range(2):
                    store_g(i * 2 + k, k)
            store_g(LAST, 0)

            sp.wait_ge(s_slow, 1)
            slow = sp.to_reg(sp.value_load(slowi[0:1, 0:1], min_val=0, max_val=1))
            sp.wait_ge(s_run, 32 * NG)
            with sp.If_ne(slow, 0):
                for k in range(2):
                    sp.dma_start(srt[k * LL:(k + 1) * LL, :].rearrange("(p t) o -> p (t o)", p=P), zeros).then_inc(s_zdma, 16)
                for k in range(2):
                    sp.wait_ge(s_scat[k], 32 * EC // 2)

            def lists(lo, hi, sem):
                for k in range(2):
                    d = srec[:, k, lo * TQ:hi * TQ].rearrange("p (b t) -> p b t", t=TQ)
                    a = srt[k * LL + lo * PB:k * LL + hi * PB, :].rearrange("(b q) o -> b (q o)", q=PB)
                    sp.dma_start(d[:, :, 0:TS], a[:, 0:TS * P].rearrange("b (p t) -> p b t", t=TS)).then_inc(sem, 16)
                    sp.dma_start(d[:, :, TS:TQ], a[:, TS * P:TQ * P].rearrange("b (p t) -> p b t", t=1),
                                 allow_slow_non_contiguous=True).then_inc(sem, 16)

            lists(0, BF, s_srec0)
            lists(BF, NB, s_srec1)

            with sp.If_ne(slow, 0):
                sp.wait_ge(s_nov, 1)
                nov = sp.value_load(novi[0:1, 0:1], min_val=1, max_val=OV)
                with sp.Fori(0, nov) as t:
                    sp.wait_ge(s_oadd, t + 1)
                    for k in range(2):
                        sp.dma_start(orec[:, k:k + 1], srt[ds(t * P + (k * LL + NB * PB), P), :]).then_inc(s_orec, 16)
                sp.wait_ge(s_ovd, 1)
                sp.dma_start(ovs.rearrange("p b w -> p (b w)"), accf).then_inc(s_ovs, 16)
                sp.wait_ge(s_ovs, 16)
            sp.sem_inc(s_free, 1)

            def load_ov(b, k, start=False):
                if not start:
                    sp.wait_ge(s_ev, b - 1)
                sp.dma_start(ovr[:, k, :], ovs[:, ds(b, 1), :].rearrange("p o w -> p (o w)")).then_inc(s_ov[k], 16)

            with sp.If_ne(slow, 0):
                load_ov(0, 0, True)
                load_ov(1, 1, True)
                with sp.Fori(1, NB // 2) as i:
                    for k in range(2):
                        load_ov(i * 2 + k, k)
                load_ov(LAST, 0)
            with sp.If_eq(slow, 0):
                sp.sem_inc(s_ov[0], 16 * (NB // 2 + 1))
                sp.sem_inc(s_ov[1], 16 * (NB // 2))
            sp.wait_ge(s_ev, NB)
            sp.wait_ge(s_w3z, 1)
            for d, w in late:
                sp.dma_start(d, w).then_inc(s_w3, 16)

            def store_o(b, k, n=P):
                sp.wait_ge(s_os, b + 1)
                sp.dma_start(out[ds(b * P, n), :], ot[0:n, k, :]).then_inc(s_od[k], 16)

            with sp.Fori(0, NB // 2) as i:
                for k in range(2):
                    store_o(i * 2 + k, k)
            store_o(LAST, 0, TAIL)
            sp.wait_ge(s_od[0], 16 * (NB // 2 + 1))
            sp.wait_ge(s_od[1], 16 * (NB // 2))

        @block.gpsimd
        def _(pool):
            pool.iota(iota[:, :], pattern=[[1, P]], base=0, channel_multiplier=0,
                      allow_small_or_imprecise_dtypes=True).then_inc(s_const, 1)
            pool.iota(iotap[:, :], pattern=[[1, 1]], base=0, channel_multiplier=1,
                      allow_small_or_imprecise_dtypes=True).then_inc(s_const, 1)
            pool.iota(slotf[:, ECOL:EC], pattern=[[P, EC - ECOL]], base=NB * PB + OV * P, channel_multiplier=1,
                      allow_small_or_imprecise_dtypes=True).then_inc(s_const, 1)
            pool.iota(firstc[0:VB, :], pattern=[[1, 1]], base=0, channel_multiplier=PB,
                      allow_small_or_imprecise_dtypes=True).then_inc(s_const, 1)
            pool.memset(ones[:, :], 1.0).then_inc(s_const, 1)
            pool.memset(onesb[:, :], 1.0).then_inc(s_const, 1)
            pool.memset(ovr[:, :, :], 0.0).then_inc(s_const, 1)
            pool.memset(rows[:, TS, :], 0.0).then_inc(s_const, 1)

            def values(g, k, h):
                pool.wait_ge(s_flag, g + 1)
                if not (isinstance(g, int) and g == 0):
                    pool.wait_ge(s_put, g * 2 + h - 1)
                for i, t in enumerate((packf, ewf)):
                    m = pool.tensor_tensor(hot_v[h][:, :, i, :],
                                           flags4[k][:, :, h, 1:HS].rearrange("p b j -> p j b"),
                                           t[:, ds(g * GC + h * HC, HC)].unsqueeze(2).broadcast_to([P, HC, NB]), ALU.mult)
                m.then_inc(s_hv, 1)

            def send(g, k, h):
                if isinstance(g, int) and g == 0 and h == 0:
                    pool.wait_ge(s_zdma, 32)
                else:
                    pool.wait_ge(s_run, g * 32 + h * 16)
                pool.wait_ge(s_idx0, g + (1 + h))
                pool.wait_ge(s_out, g + 1)
                pool.sem_inc(s_tick, 1)
                pool.indirect_dma_start(
                    srt[:, :], bass.IndirectOffsetOnAxis(ap=idx[:, k, h:h + 1], axis=0),
                    runs[k][:, h * RUN:(h + 1) * RUN], None).then_inc(s_run, 16)

            def both(g, k, first=False):
                values(g, k, 0)
                if not first:
                    send(g - 2, k, 1)
                values(g, k, 1)
                send(g - 1, 1 - k, 0)

            pool.wait_ge(s_pack, 1)
            values(0, 0, 0)
            values(0, 0, 1)
            both(1, 1, True)
            with pool.Fori(1, NG // 2) as i:
                for k in range(2):
                    both(i * 2 + k, k)
            send(NG - 2, 0, 1)
            send(NG - 1, 1, 0)
            send(NG - 1, 1, 1)

            pool.wait_ge(s_slow, 1)
            slow = pool.to_reg(pool.value_load(slowi[0:1, 0:1], min_val=0, max_val=1))

            def scatter(i, k, start=False):
                for n, t in enumerate((packf, ewf)):
                    if n == 1 or not start:
                        pool.wait_ge(s_scat[k], i * 32 * U + n * 16 * U)
                    if n == 1:
                        pool.sem_inc(s_tick, 1)
                        pool.tensor_scalar(ring_s[:, k, :], ring_s[:, k, :], LL, None, ALU.add)
                    else:
                        pool.tensor_copy(ring_s[:, k, :], sloti[:, ds((i * 2 + k) * U, U)])
                    pool.tensor_copy(ring_r[:, k, :], t[:, ds((i * 2 + k) * U, U)]).then_inc(s_stage, 1)
                    pool.wait_ge(s_stage, (i * 2 + k) * 2 + n + 1)
                    pool.sem_inc(s_tick, 1)
                    for u in range(U):
                        pool.indirect_dma_start(
                            srt[:, :], bass.IndirectOffsetOnAxis(ap=ring_s[:, k, u:u + 1], axis=0),
                            ring_r[:, k, u:u + 1], None).then_inc(s_scat[k], 16)

            with pool.If_ne(slow, 0):
                pool.wait_ge(s_zdma, 64)
                pool.wait_ge(s_slot, 1)
                for k in range(2):
                    scatter(0, k, True)
                with pool.Fori(1, EC // (2 * U)) as i:
                    for k in range(2):
                        scatter(i, k)

            pool.wait_ge(s_gd[0], 16 * (NB // 2 + 1))
            pool.wait_ge(s_gd[1], 16 * (NB // 2))
            with pool.If_ne(slow, 0):
                pool.wait_ge(s_nov, 1)
                nov = pool.value_load(novi[0:1, 0:1], min_val=1, max_val=OV)
                pool.wait_ge(s_clear, 4)
                pool.iota(iota_t, pattern=[[1, OV]], base=0, channel_multiplier=0,
                          allow_small_or_imprecise_dtypes=True).then_inc(s_ti, 1)
                with pool.Fori(0, nov) as t:
                    pool.wait_ge(s_oidx, t + 1)
                    pool.sem_inc(s_tick, 1)
                    pool.indirect_dma_start(
                        orow, None, gtab[:, :], bass.IndirectOffsetOnAxis(ap=oidx, axis=0)).then_inc(s_orow, 16)

            pool.wait_ge(s_ovd, 1)
            pool.wait_ge(s_need, 1)
            def gather(b, k, start=False):
                pool.wait_ge(s_idx, b + 1)
                needed = pool.to_reg(pool.value_load(neededi[0:1, 0, ds(b, 1)], min_val=0, max_val=1))

                def tile(u):
                    pool.indirect_dma_start(
                        rows[:, u, :], None, gtab[:, :],
                        bass.IndirectOffsetOnAxis(ap=ring_i[:, k, u:u + 1], axis=0)).then_inc(s_row[u], 16)

                for lo, hi in zip((0,) + UG, UG):
                    if not start:
                        pool.wait_ge(s_seg, b * TQ - TQ + hi)
                        pool.sem_inc(s_tick, 1)
                    for u in range(lo, min(hi, TS)):
                        tile(u)
                with pool.If_ne(needed, 0):
                    tile(TS)

            gather(0, 0, True)
            gather(1, 1)
            with pool.Fori(1, NB // 2) as i:
                for k in range(2):
                    gather(i * 2 + k, k)
            gather(LAST, 0)

        @block.vector
        def _(dve):
            step = Chain(dve, s_dve)
            v = nc.vector

            v.memset(rowi[:, ECOL:EC], NB * P)
            v.memset(coli[:, ECOL:EC], 0)
            v.memset(ewf[:, ECOL:EC], 0.0).then_inc(s_clear, 1)
            v.memset(zeros, 0.0).then_inc(s_clear, 1)
            v.memset(res[:, LAST, :], 0.0).then_inc(s_clear, 1)
            v.memset(zcol[:, :], 0.0)
            v.memset(Ws2[:, :], 0.0).then_inc(s_zero, 1)
            v.memset(zrow[:, :], 0.0).then_inc(s_zs, 1)
            v.memset(reset, 1.0)
            step(v.memset(oneb, 1.0))
            v.memset(halved(reset)[:, :, :, 0:1], 0.0)
            dve.wait_ge(s_const, 8)
            v.tensor_scalar(ident[:, :], iota[:, :], iotap[:, 0:1], None, ALU.is_equal)
            v.tensor_scalar(lower, iota[:, :], iotap[:, 0:1], None, ALU.is_gt)
            v.tensor_scalar(lowerb, iota[:, :], iotap[:, 0:1], None, ALU.is_gt)
            step(v.tensor_copy(iotab, iota[:, :]))
            v.tensor_copy(buckets.rearrange("p b h j -> p b (h j)"), iotab[:, 0:NB].unsqueeze(2).broadcast_to([P, NB, GC]))
            v.tensor_scalar(iota1, iota[:, :], 1.0, None, ALU.add)
            v.memset(valid[:, :], 1.0)
            step(v.tensor_scalar(over[0:VB, :], iotap[0:VB, :], float(NB), float(LL - NB * PB), ALU.is_ge, ALU.mult))
            step(v.tensor_tensor(firstc[0:VB, :], firstc[0:VB, :], over[0:VB, :], ALU.add))
            v.tensor_copy(idx[:, 0, 0:1], firstc[0:VB, :]).then_inc(s_idx0, 1)
            step(v.tensor_scalar(padf[:, :], iotap[:, :], float(TAIL), None, ALU.is_ge))
            step(v.tensor_scalar(valid[:, LAST:NB], padf[:, :], -1.0, 1.0, ALU.mult, ALU.add))

            dve.wait_ge(s_edge, 96)
            step(v.tensor_scalar(sloti, rowi, 7, None, ALU.logical_shift_right))
            step(v.tensor_scalar(tmpi, rowi, P - 1, None, ALU.bitwise_and))
            step(v.tensor_copy(hif, sloti))
            step(v.tensor_copy(hib, sloti))
            step(v.scalar_tensor_tensor(tmpi, coli, 7, tmpi, ALU.logical_shift_left, ALU.bitwise_or))
            v.tensor_copy(packf, tmpi).then_inc(s_pack, 1)

            def flag(g, k):
                if not (isinstance(g, int) and g < 2):
                    dve.wait_ge(s_hv, g * 2 - 2)
                v.tensor_tensor(flags4[k][:, :, :, 1:HS],
                                hib[:, ds(g * GC, GC)].rearrange("p (h j) -> p h j", h=2).unsqueeze(1)
                                .broadcast_to([P, NB, 2, HC]),
                                buckets, ALU.is_equal).then_inc(s_flag, 1)

            def rank(g, k, ahead=None, i=None):
                start = isinstance(g, int) and g == 0
                dve.wait_ge(s_bs, g + 1)
                step(v.tensor_tensor_scan(run, reset, flags[k], 0.0, ALU.mult, ALU.add))
                if not (isinstance(g, int) and g < 2):
                    dve.wait_ge(s_tot, g)
                for h in range(2):
                    m = v.tensor_tensor(cntp[k][:, h, :, :],
                                        run4[:, :, h, HC:HS].rearrange("p b o -> p o b").broadcast_to([P, 2, NB]),
                                        flags4[k][:, :, h, 0:1].rearrange("p b o -> p o b").broadcast_to([P, 2, NB]),
                                        ALU.subtract)
                m.then_inc(s_cp, 1)
                v.tensor_tensor(halved(prod, HC), run4[:, :, :, 1:HS], flags4[k][:, :, :, 1:HS], ALU.mult).then_inc(s_prod, 1)
                if ahead is not None:
                    flag(ahead, 1 - k)
                if i is not None:
                    place(g - 1, 1 - k)
                dve.wait_ge(s_prod, g + 1)
                step(v.tensor_reduce(rankf[:, ds(g * GC, GC)], prod.rearrange("p (b j) -> p j b", j=GC), AX.X, ALU.add))
                for h in range(2):
                    if not start:
                        dve.wait_ge(s_put, g * 2 + h - 1)
                    v.tensor_tensor(hot_s[h],
                                    rankf[:, ds(g * GC + h * HC, HC)].unsqueeze(2).broadcast_to([P, HC, RUN]),
                                    iota1[:, 0:RUN].unsqueeze(1).broadcast_to([P, HC, RUN]), ALU.is_equal).then_inc(s_hs, 1)
                    if i is not None:
                        gates(i, h, isinstance(i, int) and i == 0)

            def place(g, k):
                dve.wait_ge(s_tot, g + 1)
                if not (isinstance(g, int) and g == 0):
                    dve.wait_ge(s_run, g * 32 - 16)
                v.tensor_scalar(idx[:, k, 1:2], bank[2][0:VB, 1:2], float(TQ * P), firstc[0:VB, :], ALU.min, ALU.add)
                v.tensor_scalar(idx[:, 1 - k, 0:1], bank[2][0:VB, 0:1], float(TQ * P), firstc[0:VB, :],
                                ALU.min, ALU.add).then_inc(s_idx0, 1)

            flag(0, 0)
            flag(1, 1)
            rank(0, 0)
            flag(2, 0)

            dve.wait_ge(s_w, 16 * len(wloads))
            for k in range(2):
                step(v.tensor_tensor_reduce(xn1[:, k, :], Wg[:, k, 0:F], a2b, 1.0, 0.0, ALU.mult, ALU.add,
                                            accum_out=Wg[:, k, F:GW]))
            step(v.tensor_scalar(tb[:, :], tb[:, :], 0.1, 5.0, ALU.max, ALU.min))
            step(v.reciprocal(tb[:, :], tb[:, :]))
            dve.wait_ge(s_wxs, 1)
            tbc = tb[:, :].unsqueeze(2)
            for k in range(2):
                v.tensor_tensor(Wxs[:, k, :].rearrange("p (h g) -> p h g", g=G),
                                bank[4 + k][:, :].rearrange("p (h g) -> p h g", g=G),
                                tbc.broadcast_to([P, H, G]), ALU.mult)
            step(v.tensor_tensor(bxs[:, :].rearrange("p (h g) -> p h g", g=G),
                                 bank[3][0:1, :].rearrange("p (h g) -> p h g", g=G),
                                 bsr[:, :].unsqueeze(1).broadcast_to([1, H, G]), ALU.add))
            v.tensor_tensor(bxs[:, :].rearrange("p (h g) -> p h g", g=G),
                            bxs[:, :].rearrange("p (h g) -> p h g", g=G),
                            tb[0:1, :].unsqueeze(2).broadcast_to([1, H, G]), ALU.mult).then_inc(s_wxd, 1)

            def stats(b, view):
                return v.bn_stats(st6[:, ds(b, 1), :].rearrange("p o s -> p (o s)"), view)

            def norm_stats():
                v.tensor_tensor(mean[:, :], st6[:, :, 1], st6[:, :, 4], ALU.add)
                step(v.tensor_tensor(var[:, :], st6[:, :, 1], st6[:, :, 4], ALU.subtract))
                step(v.scalar_tensor_tensor(var[:, :], var[:, :], 0.25, var[:, :], ALU.mult, ALU.mult))
                step(v.tensor_tensor(nwt[:, :], st6[:, :, 2], st6[:, :, 5], ALU.add))
                step(v.scalar_tensor_tensor(var[:, :], nwt[:, :], 1.0 / F, var[:, :], ALU.mult, ALU.add))
                step(v.tensor_scalar(var[:, :], var[:, :], EPS, None, ALU.add))
                v.tensor_scalar(nwt[:, :], var[:, :], 1.0, None, ALU.mult).then_inc(s_var, 1)
                dve.wait_ge(s_rs0, 1)
                step(v.tensor_tensor(nwt[:, :], var[:, :], rstd[:, :], ALU.mult))
                step(v.tensor_tensor(nwt[:, :], nwt[:, :], rstd[:, :], ALU.mult))
                step(v.tensor_scalar(nwt[:, :], nwt[:, :], -0.5, 1.5, ALU.mult, ALU.add))
                step(v.tensor_tensor(rstd[:, :], rstd[:, :], nwt[:, :], ALU.mult))
                v.scalar_tensor_tensor(nmr[:, :], mean[:, :], -0.5, rstd[:, :], ALU.mult, ALU.mult).then_inc(s_rs, 1)

            dve.wait_ge(s_x, 32)
            with dve.Fori(0, NB // Q) as i:
                for q in range(Q):
                    stats(i * Q + q, res[:, ds(i * Q + q, 1), :].rearrange("p o f -> p (o f)"))
            step(v.tensor_copy(part[:, 0:1], iota[:, 0:1]))
            norm_stats()
            place(0, 0)
            rank(1, 1)

            def gate(b, k, first):
                dve.wait_ge(s_gx, b + 1)
                step(v.tensor_scalar(sm[:, k, 1:2], sm[:, k, 0:1], 1.0, None, ALU.add))
                if not first:
                    dve.wait_ge(s_gd[k], (b - k) * 8)
                v.reciprocal(Gt[:, k, F:GW], sm[:, k, 1:2]).then_inc(s_gr, 1)

            def gates(i, h, first):
                if h == 0:
                    dve.wait_ge(s_gx, i * 2 + 2)
                    v.tensor_scalar(sm[:, :, 1:2], sm[:, :, 0:1], 1.0, None, ALU.add).then_inc(s_g1, 1)
                    return
                if not first:
                    for k in range(2):
                        dve.wait_ge(s_gd[k], i * 16)
                dve.wait_ge(s_g1, i + 1)
                v.reciprocal(Gt[:, :, F:GW], sm[:, :, 1:2]).then_inc(s_gr, 2)

            def both(g, k, i, last=False):
                if i is None:
                    place(g - 1, 1 - k)
                rank(g, k, None if last else g + 1, None if i is None else i - 1)

            both(G0, 0, None)
            both(G0 + 1, 1, 1)
            n0 = step.n
            with dve.Fori(1, (NG - G0) // 2 - 1) as i:
                step.enter(i, 1, 2 * 2)
                for k in range(2):
                    both(i * 2 + (G0 + k), k, i * 2 + k)
            assert step.n - n0 == 2 * 2
            step.leave((NG - G0) // 2 - 2, 2 * 2)
            both(NG - 2, 0, NG - 2 - G0)
            both(NG - 1, 1, NG - 1 - G0, True)
            place(NG - 1, 1)

            step(v.tensor_reduce(part[:, 0:1], rankf, AX.X, ALU.max))
            step(v.tensor_scalar(part[:, 1:2], part[:, 0:1], float(RUN), None, ALU.is_gt))
            step(v.tensor_scalar(part[0:VB, 2:3], bank[2][0:VB, 0:1], float(TQ * P), None, ALU.is_gt))
            v.tensor_tensor(part[0:VB, 1:2], part[0:VB, 1:2], part[0:VB, 2:3], ALU.max)
            step(v.memset(part[:, 4:5], 0.0))
            v.tensor_scalar(part[0:NB, 4:5], bank[2][0:NB, 0:1], float(TS * P), None, ALU.is_gt).then_inc(s_long, 1)
            dve.wait_ge(s_longt, 1)
            step(v.tensor_reduce(part[0:1, 3:4], bank[0][0:1, 0:P], AX.X, ALU.max))
            v.tensor_copy(slowi[:, :], part[0:1, 3:4]).then_inc(s_slow, 1)
            v.memset(neededf[:, 0:1], 1.0)
            step(v.tensor_scalar(neededf[:, 1:NB], bank[0][0:1, P + 1:P + NB], part[0:1, 3:4], None, ALU.max))
            v.tensor_copy(neededi[:, 0, :], neededf)
            step(v.tensor_tensor_scan(sumf, ones[0:1, 0:NB], neededf, 0.0, ALU.mult, ALU.add))
            v.tensor_scalar(neededi[:, 1, :], sumf, 16.0, None, ALU.mult).then_inc(s_need, 1)
            dve.wait_ge(s_slow, 1)
            slow = dve.to_reg(dve.value_load(slowi[0:1, 0:1], min_val=0, max_val=1))

            for h in range(2):
                gates(NB // 2 - 1, h, False)
            gate(LAST, 0, False)

            with dve.If_ne(slow, 0):
                gstep = Chain(dve, s_gen)
                dve.wait_ge(s_run, 32 * NG)
                v.memset(accf, 0.0)
                gstep(v.memset(slotf[:, 0:ECOL], 0.0))
                with dve.Fori(0, NB // Q) as i:
                    gstep.enter(i, 0, Q + 1)
                    for q in range(Q):
                        gstep(v.tensor_scalar(scan, hif, iota[:, ds(i * Q + q, 1)], 0.0, ALU.is_equal, ALU.add,
                                              accum_out=part[:, q:q + 1]))
                    gstep(v.tensor_copy(cnt[:, ds(i * Q, Q)], part[:, :]))
                gstep.leave(NB // Q, Q + 1)
                dve.sem_inc(s_cnt, 1)
                gstep(v.tensor_scalar(first[:, :], iota[:, 0:NB], float(PB), None, ALU.mult))
                gstep(v.tensor_scalar(limit[:, :], first[:, :], float(TQ * P), None, ALU.add))
                dve.wait_ge(s_pre, 1)
                gstep(v.tensor_scalar(ntf[:, :], bank[0][:, 64:64 + NB], float(-TQ * P), 0.0, ALU.add, ALU.max))
                gstep(v.tensor_scalar(nti[:, :], ntf[:, :], float(P - 1), None, ALU.add))
                gstep(v.tensor_scalar(nti[:, :], nti[:, :], 7, None, ALU.logical_shift_right))
                gstep(v.tensor_copy(ntf[:, :], nti[:, :]))
                gstep(v.tensor_tensor_scan(ctf[:, :], ones[:, 0:NB], ntf[:, :], 0.0, ALU.mult, ALU.add))
                gstep(v.tensor_tensor(jump[:, :], ctf[:, :], ntf[:, :], ALU.subtract))
                gstep(v.tensor_scalar(jump[:, :], jump[:, :], float(P), float(NB * PB), ALU.mult, ALU.add))
                gstep(v.tensor_tensor(jump[:, :], jump[:, :], limit[:, :], ALU.subtract))
                gstep(v.tensor_tensor(base[:, :], first[:, :], bank[0][:, 0:NB], ALU.add))
                gstep(v.tensor_scalar(base[:, :], base[:, :], -1.0, None, ALU.add))
                v.tensor_scalar(novi[:, :], ctf[0:1, NB - 1:NB], 1.0, None, ALU.max).then_inc(s_nov, 1)
                dve.wait_ge(s_nov, 1)
                with dve.Fori(0, NB) as b:
                    gstep.enter(b, 0, 6)
                    gstep(v.tensor_scalar(mask[:, :], hif, iota[:, ds(b, 1)], None, ALU.is_equal))
                    gstep(v.tensor_tensor_scan(scan, onesb[:, :], mask[:, :], base[:, ds(b, 1)], ALU.mult, ALU.add))
                    dve.sem_inc(s_tick, 1)
                    gstep(v.copy_predicated(slotf, mask[:, :], scan))
                    gstep(v.tensor_scalar(scan, slotf, limit[:, ds(b, 1)], jump[:, ds(b, 1)], ALU.is_ge, ALU.mult))
                    gstep(v.scalar_tensor_tensor(scan, hif, iota[:, ds(b, 1)], scan, ALU.is_equal, ALU.mult))
                    gstep(v.tensor_tensor(slotf, slotf, scan, ALU.add))
                gstep.leave(NB, 6)
                v.tensor_copy(sloti, slotf).then_inc(s_slot, 1)


            with dve.If_ne(slow, 0):
                nov = dve.value_load(novi[0:1, 0:1], min_val=1, max_val=OV)
                dve.wait_ge(s_slot, 1)
                v.memset(ge, 0.0).then_inc(s_clear, 1)
                dve.wait_ge(s_ti, 1)
                dve.wait_ge(s_ctc, 1)
                v.tensor_copy(ctcol[:, :], bank[0][0:NB, 128:129]).then_inc(s_ge, 1)
                dve.wait_ge(s_ge, 1)
                v.tensor_scalar(ge[0:NB, :], iota_t[0:NB, :], ctcol[:, 0:1], None, ALU.is_ge).then_inc(s_ge, 1)
                dve.wait_ge(s_gs, 1)
                for c in range(2):
                    w = OV // 2
                    v.tensor_scalar(ge[0:1, c * w:(c + 1) * w], bank[1 + c][0:1, 0:w], float(LAST), float(GW),
                                    ALU.min, ALU.mult).then_inc(s_ge, 1)
                dve.wait_ge(s_ge, 4)
                v.tensor_copy(offi[0:1, :], ge[0:1, :]).then_inc(s_off, 1)
                dve.wait_ge(s_off, 1)
                v.memset(orow, 0.0).then_inc(s_oadd, 1)
                dve.wait_ge(s_oadd, 1)
                with dve.Fori(0, nov) as t:
                    dve.wait_ge(s_orec, t * 32 + 32)
                    v.tensor_copy(oreci, orec[:, 0:1]).then_inc(s_oS, 1)
                    dve.wait_ge(s_oS, t * 4 + 1)
                    v.tensor_scalar(oidx, oreci, 7, None, ALU.logical_shift_right).then_inc(s_oidx, 1)
                    v.tensor_scalar(olo[:, 0:1], oreci, P - 1, None, ALU.bitwise_and).then_inc(s_oS, 1)
                    dve.wait_ge(s_oS, t * 4 + 2)
                    v.tensor_copy(olof, olo[:, 0:1]).then_inc(s_oS, 1)
                    dve.wait_ge(s_oS, t * 4 + 3)
                    v.tensor_scalar(oS, iota[:, :], olof, orec[:, 1:2], ALU.is_equal, ALU.mult).then_inc(s_oS, 1)
                    off = dve.value_load(offi[0:1, ds(t, 1)], min_val=0, max_val=LAST * GW)
                    dve.wait_ge(s_oseg, t + 1)
                    v.tensor_tensor(accf[:, ds(off, GW)], accf[:, ds(off, GW)], bank[0][:, 0:GW], ALU.add).then_inc(s_oadd, 1)
                    dve.wait_ge(s_oadd, t + 2)
            step(v.tensor_copy(part[:, :], iota[:, 0:Q]))
            v.tensor_copy(var[:, 0:Q], part[:, :]).then_inc(s_ovd, 1)

            dve.wait_ge(s_srec0, 64)

            def decode(b, k):
                r = pki[:, :]
                step(v.tensor_copy(r, srec[:, 0, ds(b * TQ, TQ)]))
                step(v.tensor_scalar(loi[:, :], r, P - 1, None, ALU.bitwise_and))
                v.tensor_copy(lof[:, k, :], loi[:, :])
                v.tensor_scalar(ring_i[:, k, :], r, 7, None, ALU.logical_shift_right).then_inc(s_idx, 1)
                dve.wait_ge(s_idx, b + 1)

            def select(b, k, lo, hi, start=False):
                for u in range(lo, hi):
                    if not start:
                        dve.wait_ge(s_seg, b * TQ - TQ + u + 1)
                    v.tensor_scalar(S[:, u, :], iota[:, :], lof[:, k, u:u + 1], srec[:, 1, ds(b * TQ + u, 1)],
                                    ALU.is_equal, ALU.mult).then_inc(s_S, 1)

            def feat(b):
                return res[:, ds(b, 1), :].rearrange("p o f -> p (o f)")

            def take(b, k, last):
                dve.wait_ge(s_seg, b * TQ + TQ)
                dve.wait_ge(s_ov[k], (b - k) * 8 + 16)
                v.tensor_tensor(ag[:, :], bank[k][:, 0:GW], ovr[:, k, :], ALU.add).then_inc(s_ev, 1)
                dve.wait_ge(s_ev, b + 1)
                if last:
                    step(v.tensor_tensor(ag[:, F:GW], ag[:, F:GW], padf[:, :], ALU.add))

            def gnn(b):
                step(v.reciprocal(col(RI), ag[:, F:GW]))
                step(v.scalar_tensor_tensor(neg[:, :], ag[:, 0:F], col(RI), a1b[:, :], ALU.mult, ALU.mult,
                                            accum_out=col(ZD)))
                v.scalar_tensor_tensor(col(ZA), col(ZD), -1.0, col(ZD), ALU.mult, ALU.min).then_inc(s_z1, 1)
                step(v.tensor_scalar(neg[:, :], ag[:, 0:F], col(RI), 0.0, ALU.mult, ALU.min))
                dve.wait_ge(s_l1, b * 2 + 2)
                v.scalar_tensor_tensor(col(LD), col(ZD), 0.0, col(LG), ALU.max, ALU.add).then_inc(s_l2, 1)
                dve.wait_ge(s_rel, b + 1)
                step(v.tensor_tensor(pos[:, :], pos[:, :], feat(b), ALU.add))
                dve.wait_ge(s_ex, b + 1)
                v.scalar_tensor_tensor(feat(b), neg[:, :], -1.0, pos[:, :], ALU.add, ALU.add).then_inc(s_x1, 1)
                dve.wait_ge(s_x1, b + 1)
                dve.sem_inc(s_tick, 1)
                step(v.bn_stats(bst[:, :], feat(b)))
                dve.sem_inc(s_tick, 1)
                step(v.bn_aggr(bmv[:, :], bst[:, :]))
                v.tensor_scalar(col(VA), bmv[:, 1:2], EPS, None, ALU.add).then_inc(s_var, 1)
                dve.wait_ge(s_rs0, b + 2)
                step(v.scalar_tensor_tensor(col(NW), col(VA), col(RS), col(RS), ALU.mult, ALU.mult))
                step(v.tensor_scalar(col(NW), col(NW), -0.5, 1.5, ALU.mult, ALU.add))
                step(v.tensor_tensor(col(RS), col(RS), col(NW), ALU.mult))
                v.scalar_tensor_tensor(col(NM), bmv[:, 0:1], -1.0, col(RS), ALU.mult, ALU.mult).then_inc(s_rs, 1)

            def heads(t):
                return t.rearrange("p (h g) -> p h g", g=G)

            def softmax(b, start=False):
                dve.wait_ge(s_lm, b + 1)
                step(v.tensor_reduce(hm[:, 0, :], heads(bank[4][:, :]), AX.X, ALU.max))
                v.tensor_tensor(heads(lg[:, :]), heads(bank[4][:, :]),
                                hm[:, 0, :].unsqueeze(2).broadcast_to([P, H, G]), ALU.subtract).then_inc(s_ls, 1)
                dve.wait_ge(s_le, b + 1)
                step(v.tensor_reduce(hm[:, 1, :], heads(lg[:, :]), AX.X, ALU.add))
                step(v.reciprocal(hm[:, 2, :], hm[:, 1, :]))
                if not start:
                    dve.wait_ge(s_M, b)
                v.tensor_tensor(heads(sw[:, :]), heads(lg[:, :]),
                                hm[:, 2, :].unsqueeze(2).broadcast_to([P, H, G]), ALU.mult).then_inc(s_sw, 1)

            def main(b, k, left, start=False):
                if left >= 1:
                    select(b + 1, 1 - k, AH, TQ)
                take(b, k, left == 0)
                if left >= 2:
                    decode(b + 2, k)
                gnn(b)
                if left >= 2:
                    select(b + 2, k, 0, AH)
                if left == 0:
                    v.memset(W3[:, :, :], 0.0).then_inc(s_w3z, 1)
                softmax(b, start)

            decode(0, 0)
            decode(1, 1)
            select(0, 0, 0, TQ, True)
            select(1, 1, 0, AH)
            n0 = step.n
            main(0, 0, 2, True)
            main(1, 1, 2)
            per = step.n - n0
            dve.wait_ge(s_srec1, 64)
            with dve.Fori(1, NB // 2 - 1) as i:
                step.enter(i, 1, per)
                for k in range(2):
                    main(i * 2 + k, k, 2)
            step.leave(NB // 2 - 2, per)
            main(NB - 3, 0, 2)
            main(NB - 2, 1, 1)
            main(NB - 1, 0, 0)

            for t in (tokd, qd, vd, ad):
                v.memset(t[:, :, :], 0.0)
            dve.wait_ge(s_M, NB)
            step(v.tensor_scalar(nrm[:, 0, :], bank[5][:, 0:NP2], 1e-5, None, ALU.add))
            v.reciprocal(nrm[:, 1, :], nrm[:, 0, :]).then_inc(s_mn, 1)
            dve.wait_ge(s_mn, 1)
            step(v.tensor_tensor(nrm[:, 2, :], bank[5][:, 0:NP2], nrm[:, 1, :], ALU.mult))
            for c in range(2):
                m = v.tensor_scalar(Mn[:, c, :], bank[2 + c // 2][:, (c % 2) * F:(c % 2 + 1) * F], nrm[:, 1, c:c + 1], None,
                                    ALU.mult)
            m.then_inc(s_mic, 1)
            mid = [0]

            def waitmid():
                mid[0] += 1
                dve.wait_ge(s_mid, mid[0])

            waitmid()
            v.tensor_copy(MnT[:, 0, :], bank[4][:, :])
            v.tensor_copy(nbT, bank[6][0:1, :]).then_inc(s_mic, 1)

            def halves(dst, psum, last=None):
                w = psum.rearrange("p (c n) -> p c n", n=P)
                v.tensor_copy(dst[0:G, :, 0:G], w[0:G, :, 0:G])
                return v.tensor_copy(dst[G:P, :, G:P], w[G:P, :, G:P])

            waitmid()
            halves(tokd, bank[7][:, :])
            w7 = bank[7][:, :].rearrange("p (c n) -> p c n", n=P)
            v.tensor_copy(tokc[0:G, :, :], w7[0:G, :, 0:G])
            v.tensor_copy(tokc[G:P, :, :], w7[G:P, :, G:P]).then_inc(s_mic, 1)
            waitmid()
            halves(qd, bank[4][:, :]).then_inc(s_mic, 1)
            waitmid()
            sc = bank[7][:, 0:NP2 * G].rearrange("p (c n) -> p c n", n=G)
            step(v.tensor_reduce(nrm[:, 0, :], sc, AX.X, ALU.max))
            v.tensor_tensor(al[:, :, :], sc, nrm[:, 0, :].unsqueeze(2).broadcast_to([P, NP2, G]),
                            ALU.subtract).then_inc(s_mic, 1)
            dve.wait_ge(s_mia, 1)
            step(v.tensor_reduce(nrm[:, 1, :], al[:, :, :], AX.X, ALU.add))
            step(v.reciprocal(nrm[:, 2, :], nrm[:, 1, :]))
            for lo in (0, G):
                m = v.tensor_tensor(ad[lo:lo + G, :, lo:lo + G], al[lo:lo + G, :, :],
                                    nrm[lo:lo + G, 2, :].unsqueeze(2).broadcast_to([G, NP2, G]), ALU.mult)
            m.then_inc(s_mic, 1)
            waitmid()
            v.tensor_copy(aT[:, :, :], bank[4][:, :].rearrange("p (c n) -> p c n", n=P)).then_inc(s_mic, 1)
            waitmid()
            v.tensor_copy(oT[:, :, :], bank[5][:, :].rearrange("p (c n) -> p c n", n=P)).then_inc(s_mic, 1)
            waitmid()
            step(v.tensor_copy(Pm[:, 0:2, :], bank[6][:, :].rearrange("p (c f) -> p c f", f=F)))
            v.tensor_tensor(Pm[0:G, 0, :], Pm[0:G, 0, :], bob, ALU.add).then_inc(s_mic, 1)

            def result(b, k, first):
                dve.wait_ge(s_o, b + 1)
                if not first:
                    dve.wait_ge(s_od[k], (b - k) * 8)
                v.tensor_tensor(ot[:, k, :], bank[4 + k][:, 0:F], feat(b), ALU.add).then_inc(s_os, 1)

            result(0, 0, True)
            result(1, 1, True)
            with dve.Fori(1, NB // 2) as i:
                for k in range(2):
                    result(i * 2 + k, k, False)
            result(LAST, 0, False)

        @block.scalar
        def _(act):
            a = nc.scalar
            a.preload_act_table_set("natural_log_exp_and_others")
            step = Chain(act, s_act)

            def guess(n, d, t, v):
                act.wait_ge(s_var, n)
                step(a.activation(t, v, ACT.Ln))
                a.activation(d, t, ACT.Exp, scale=-0.5).then_inc(s_rs0, 1)

            def front(g, k):
                act.wait_ge(s_base, g + 1)
                if not (isinstance(g, int) and g < 2):
                    act.wait_ge(s_cp, g - 1)
                a.copy(flags4[k][:, :, :, 0], bank[0][:, 0:2 * NB].rearrange("p (b h) -> p b h", h=2)).then_inc(s_bs, 1)

            def runs_out(g, k):
                act.wait_ge(s_put, g * 2 + 2)
                if not (isinstance(g, int) and g < 2):
                    act.wait_ge(s_run, g * 32 - 32)
                a.copy(runs[k], bank[1 + 4 * k][0:VB, 0:2 * RUN]).then_inc(s_out, 1)

            def xnorm(b, k, first):
                if not first:
                    act.wait_ge(s_xt, b - 1)
                a.activation(xn1[:, k, :], res[:, ds(b, 1), :].rearrange("p o f -> p (o f)"), ACT.Identity,
                             bias=nmr[:, ds(b, 1)], scale=rstd[:, ds(b, 1)]).then_inc(s_xn, 1)

            def xtrans(b, k, first):
                act.wait_ge(s_xt, b + 1)
                if not first:
                    act.wait_ge(s_gm, b - 1)
                a.copy(xT1[:, k, :], bank[6 + k][:, 0:F]).then_inc(s_xc, 1)

            def gate(b, k, first):
                act.wait_ge(s_gm, b + 1)
                if not first:
                    act.wait_ge(s_gr, b - 1)
                a.activation(sm[:, k, 0:1], bank[3 + k][:, F:GW], ACT.Exp, scale=-1.0).then_inc(s_gx, 1)

            def gated(b, k):
                act.wait_ge(s_gr, b + 1)
                a.activation(Gt[:, k, 0:F], bank[3 + k][:, 0:F], ACT.Identity, bias=zcol[:, 0:1],
                             scale=Gt[:, k, F:GW]).then_inc(s_gt, 1)

            def both(g, k, i, last=False):
                first = isinstance(i, int) and i == 0
                if not first:
                    for j in range(2):
                        gate(i * 2 - 2 + j, j, isinstance(i, int) and i == 1)
                for j in range(2):
                    xnorm(i * 2 + j, j, first)
                if not last:
                    front(g + 1, 1 - k)
                runs_out(g - 1, 1 - k)
                for j in range(2):
                    xtrans(i * 2 + j, j, first)
                for j in range(2):
                    if not first:
                        gated(i * 2 - 2 + j, j)

            front(0, 0)
            front(1, 1)

            for k in range(2):
                act.wait_ge(s_wxt, k + 1)
                a.copy(WxT[:, :, k * P:(k + 1) * P], bank[6 + k][:, :].rearrange("p (c n) -> p c n", n=P)).then_inc(s_wxc, 1)

            runs_out(0, 0)
            front(2, 0)
            guess(1, rstd[:, :], lnv[:, :], nwt[:, :])
            act.wait_ge(s_rs, 1)
            both(G0, 0, 0)
            both(G0 + 1, 1, 1)
            with act.Fori(1, (NG - G0) // 2 - 1) as i:
                for k in range(2):
                    both(i * 2 + (G0 + k), k, i * 2 + k)
            both(NG - 2, 0, NG - 2 - G0)
            both(NG - 1, 1, NG - 1 - G0, True)
            for j in range(2):
                gate(NB - 3 + j, j, False)
            runs_out(NG - 1, 1)
            xnorm(LAST, 0, False)
            for j in range(2):
                gated(NB - 3 + j, j)
            xtrans(LAST, 0, False)
            gate(LAST, 0, False)
            gated(LAST, 0)

            def main(b, start=False):
                act.wait_ge(s_z1, b + 1)
                a.activation(col(EX), col(ZA), ACT.Exp).then_inc(s_l1, 1)
                act.wait_ge(s_l1, b * 2 + 1)
                a.activation(col(LG), col(EX), ACT.Ln, bias=1.0).then_inc(s_l1, 1)
                if not start:
                    act.wait_ge(s_x1, b)
                a.activation(pos[:, :], ag[:, 0:F], ACT.Relu, scale=col(RI)).then_inc(s_rel, 1)
                act.wait_ge(s_l2, b + 1)
                a.activation(neg[:, :], neg[:, :], ACT.Exp, scale=col(LD)).then_inc(s_ex, 1)
                step.n = 1
                step.loop = b
                guess(b + 2, col(RS), col(LV), col(VA))
                act.wait_ge(s_rs, b + 2)
                if not start:
                    act.wait_ge(s_M, b)
                a.activation(xn[:, :], res[:, ds(b, 1), :].rearrange("p o f -> p (o f)"), ACT.Identity,
                             bias=col(NM), scale=col(RS)).then_inc(s_xn, 1)
                if not start:
                    keep(b - 1)
                act.wait_ge(s_xt, b + NB + 1)
                if not start:
                    act.wait_ge(s_lm, b)
                a.copy(xT[:, :], bank[6][:, 0:F]).then_inc(s_xc, 1)
                act.wait_ge(s_ls, b + 1)
                a.activation(lg[:, :], lg[:, :], ACT.Exp).then_inc(s_le, 1)

            def keep(b):
                act.wait_ge(s_wt, b + 1)
                a.copy(swt[:, :, ds(b * P, P)], bank[7][:, :].rearrange("p (c n) -> p c n", n=P)).then_inc(s_wc, 1)

            act.wait_ge(s_free, 1)
            act.wait_ge(s_ovd, 1)
            main(0, True)
            with act.Fori(1, NB) as b:
                main(b)
            keep(LAST)

            act.wait_ge(s_mn, 1)
            for c in range(2, NP2):
                m = a.activation(Mn[:, c, :], bank[3][:, (c % 2) * F:(c % 2 + 1) * F], ACT.Identity, bias=zcol[:, 0:1],
                                 scale=nrm[:, 1, c:c + 1])
            m.then_inc(s_ma, 1)
            act.wait_ge(s_mid, 1)
            a.copy(MnT[:, 1, :], bank[5][:, :]).then_inc(s_ma, 1)
            act.wait_ge(s_mid, 3)
            a.copy(kc[:, :, :], bank[5][:, 0:NP2 * G].rearrange("p (c n) -> p c n", n=G))
            v6 = bank[6][:, :].rearrange("p (c n) -> p c n", n=P)
            a.copy(vd[0:G, :, 0:G], v6[0:G, :, 0:G])
            a.copy(vd[G:P, :, G:P], v6[G:P, :, G:P]).then_inc(s_ma, 1)

            act.wait_ge(s_mic, 5)
            a.activation(al[:, :, :], al[:, :, :], ACT.Exp, scale=SCALE).then_inc(s_mia, 1)

            act.wait_ge(s_mid, 7)
            a.copy(Pm[:, 2:4, :], bank[7][:, :].rearrange("p (c f) -> p c f", f=F)).then_inc(s_ma, 1)

            def load(b, k, first):
                if not first:
                    act.wait_ge(s_o, b - 1)
                a.copy(stg[:, k, :].rearrange("p (c n) -> p c n", n=P), swt[:, :, ds(b * P, P)]).then_inc(s_wl, 1)

            load(0, 0, True)
            load(1, 1, True)
            with act.Fori(1, NB // 2) as i:
                for k in range(2):
                    load(i * 2 + k, k, False)
            load(LAST, 0, False)

        @block.tensor
        def _(pe):
            def mm(o, l, r, start=True, stop=True):
                return nc.tensor.matmul(o, l, r, start=start, stop=stop, skip_group_check=True)

            def above(g, k):
                pe.wait_ge(s_flag, g + 1)
                if not (isinstance(g, int) and g == 0):
                    pe.wait_ge(s_bs, g)
                for j in range(HC):
                    m = mm(bank[0][:, 0:VB], lowerb, flags4[k][:, :, :, 1 + j], j == 0, j == HC - 1)
                m.then_inc(s_base, 1)

            def put(g, k, h):
                pe.wait_ge(s_hv, g * 2 + h + 1)
                pe.wait_ge(s_hs, g * 2 + h + 1)
                if h == 0 and not (isinstance(g, int) and g < 2):
                    pe.wait_ge(s_out, g - 1)
                for j in range(HC):
                    m = mm(bank[1 + 4 * k][0:VB, h * RUN:(h + 1) * RUN], hot_v[h][:, j, :, :].rearrange("p v b -> p (v b)"),
                           hot_s[h][:, j, :], j == 0, j == HC - 1)
                m.then_inc(s_put, 1)

            def add(lo, hi, k, h, start=False):
                return mm(bank[2][0:VB, lo:hi], cntp[k][:, h, :, :].rearrange("p v b -> p (v b)"),
                          oneb[:, lo:hi], start, False)

            def total(g, k):
                pe.wait_ge(s_cp, g + 1)
                if not (isinstance(g, int) and g == 0):
                    pe.wait_ge(s_idx0, g + 1)
                    add(1, 2, 1 - k, 1)
                add(0, 2, k, 0, isinstance(g, int) and g == 0)
                add(0, 1, k, 1).then_inc(s_tot, 1)

            def transposes(n, src, ps):
                pe.wait_ge(s_xn, n + 1)
                for c in range(2):
                    t = nc.tensor.transpose(ps[:, c * P:(c + 1) * P], src[:, c * P:(c + 1) * P], ident[:, :])
                t.then_inc(s_xt, 1)

            def xtrans(b, k, first):
                if not first:
                    pe.wait_ge(s_xc, b - 1)
                transposes(b, xn1[:, k, :], bank[6 + k])

            def support(b, k, first):
                pe.wait_ge(s_xc, b + 1)
                if not first:
                    pe.wait_ge(s_gt, b - 1)
                mm(bank[3 + k][:, 0:GW], xT1[:, k, 0:P], Wg[:, 0, :], True, False)
                mm(bank[3 + k][:, 0:GW], xT1[:, k, P:F], Wg[:, 1, :], False, True).then_inc(s_gm, 1)

            def both(g, k, i, last=False):
                first = isinstance(i, int) and i == 0
                if not last:
                    above(g + 1, 1 - k)
                for j in range(2):
                    xtrans(i * 2 + j, j, first)
                total(g, k)
                put(g, k, 0)
                put(g, k, 1)
                for j in range(2):
                    support(i * 2 + j, j, first)

            pe.wait_ge(s_dve, 2)
            above(0, 0)
            above(1, 1)

            pe.wait_ge(s_w, 16 * len(wloads))
            for k in range(2):
                for c in range(NP2):
                    t = nc.tensor.transpose(bank[6 + k][:, c * P:(c + 1) * P], Wxr[:, k, c // 2, (c % 2) * P:(c % 2 + 1) * P], ident[:, :])
                t.then_inc(s_wxt, 1)
            pe.wait_ge(s_wxc, 2)
            for c in range(NP2):
                for k in range(2):
                    mm(bank[4 + k][:, c * P:(c + 1) * P], WxT[:, c, k * P:(k + 1) * P], Ws2[:, :])
                m = mm(bank[3][0:1, c * P:(c + 1) * P], bxc[:, c:c + 1], Ws2[:, :])
            m.then_inc(s_wxs, 1)

            total(0, 0)
            put(0, 0, 0)
            put(0, 0, 1)
            above(2, 0)
            total(1, 1)
            pe.wait_ge(s_wxd, 1)
            put(1, 1, 0)
            put(1, 1, 1)
            both(G0, 0, 0)
            both(G0 + 1, 1, 1)
            with pe.Fori(1, (NG - G0) // 2 - 1) as i:
                for k in range(2):
                    both(i * 2 + (G0 + k), k, i * 2 + k)
            both(NG - 2, 0, NG - 2 - G0)
            both(NG - 1, 1, NG - 1 - G0, True)
            pe.wait_ge(s_long, 1)
            nc.tensor.transpose(bank[0][0:1, 0:P], part[:, 1:2], ident[:, :])
            nc.tensor.transpose(bank[0][0:1, P:2 * P], part[:, 4:5], ident[:, :]).then_inc(s_longt, 1)
            xtrans(LAST, 0, False)
            support(LAST, 0, False)

            pe.wait_ge(s_slow, 1)
            slow = pe.to_reg(pe.value_load(slowi[0:1, 0:1], min_val=0, max_val=1))
            with pe.If_ne(slow, 0):
                pe.wait_ge(s_cnt, 1)
                mm(bank[0][:, 0:NB], lower, cnt[:, :])
                mm(bank[0][:, 64:64 + NB], ones[:, :], cnt[:, :]).then_inc(s_pre, 1)

                pe.wait_ge(s_nov, 1)
                nov = pe.value_load(novi[0:1, 0:1], min_val=1, max_val=OV)
                mm(bank[0][0:NB, 128:129], ctf[0:1, :], ones[0:1, 0:1]).then_inc(s_ctc, 1)
                pe.wait_ge(s_ge, 2)
                for c in range(2):
                    w = OV // 2
                    m = mm(bank[1 + c][0:1, 0:w], ones[0:NB, 0:1], ge[0:NB, c * w:(c + 1) * w])
                m.then_inc(s_gs, 1)
                pe.wait_ge(s_off, 1)
                with pe.Fori(0, nov) as t:
                    pe.wait_ge(s_orow, t * 16 + 16)
                    pe.wait_ge(s_oS, t * 4 + 4)
                    pe.wait_ge(s_oadd, t + 1)
                    mm(bank[0][:, 0:GW], oS, orow).then_inc(s_oseg, 1)

            pe.wait_ge(s_zs, 1)
            pe.wait_ge(s_need, 1)
            pe.wait_ge(s_gt, NB)
            pe.wait_ge(s_wxd, 1)
            pe.wait_ge(s_ovd, 1)
            for c in (2, 3, 5):
                mm(bank[c][:, :], zrow[0:1, 0:P], bxs[:, :], True, False)

            def segment(b, k, lo, hi, start=False):
                for u in range(lo, hi):
                    if u < TS:
                        pe.wait_ge(s_row[u], b * 16 + 16)
                    else:
                        pe.wait_ge(s_row[u], pe.value_load(neededi[0:1, 1, ds(b, 1)], min_val=16, max_val=16 * NB))
                    pe.wait_ge(s_S, b * TQ + u + 1)
                    if u == 0 and not start:
                        pe.wait_ge(s_ev, b - 1)
                    mm(bank[k][:, 0:GW], S[:, u, :], rows[:, u, :], u == 0, u == TQ - 1).then_inc(s_seg, 1)

            def logits(b, start=False):
                if not start:
                    pe.wait_ge(s_ls, b)
                mm(bank[4][:, :], ones[0:1, :], bxs[:, :], True, False)
                pe.wait_ge(s_xc, b + NB + 1)
                mm(bank[4][:, :], xT[:, 0:P], Wxs[:, 0, :], False, False)
                mm(bank[4][:, :], xT[:, P:F], Wxs[:, 1, :], False, True).then_inc(s_lm, 1)

            def sums(b, start=False):
                pe.wait_ge(s_sw, b + 1)
                if not start:
                    pe.wait_ge(s_wc, b)
                for c in range(NP2):
                    t = nc.tensor.transpose(bank[7][:, c * P:(c + 1) * P], sw[:, c * P:(c + 1) * P], ident[:, :])
                t.then_inc(s_wt, 1)
                for c in range(NP2):
                    w = sw[:, c * P:(c + 1) * P]
                    mm(bank[2 + c // 2][:, (c % 2) * F:(c % 2 + 1) * F], w, xn[:, :], False, False)
                    m = mm(bank[5][:, c:c + 1], w, valid[:, ds(b, 1)], False, False)
                m.then_inc(s_M, 1)

            def main(b, k, left, start=False, second=False):
                if left:
                    segment(b + 1, 1 - k, 0, 4, start)
                if not start:
                    sums(b - 1, second)
                if left:
                    segment(b + 1, 1 - k, 4, 10)
                transposes(b + NB, xn[:, :], bank[6][:, 0:F])
                if left:
                    segment(b + 1, 1 - k, 10, 12)
                logits(b, start)
                if left:
                    segment(b + 1, 1 - k, 12, TQ)

            segment(0, 0, 0, TQ, True)
            main(0, 0, True, True)
            main(1, 1, True, False, True)
            with pe.Fori(1, NB // 2) as i:
                for k in range(2):
                    main(i * 2 + k, k, True)
            main(LAST, 0, False)
            sums(LAST)

            mic = [0]
            ma = [0]

            def waitmic(n=1, act=0):
                mic[0] += n
                pe.wait_ge(s_mic, mic[0])
                if act:
                    ma[0] += act
                    pe.wait_ge(s_ma, ma[0])

            pe.wait_ge(s_wc, NB)
            pe.wait_ge(s_w3, 16 * len(late))
            waitmic(1, 1)
            for c in range(NP2):
                for f in range(2):
                    nc.tensor.transpose(bank[4 + f][:, c * P:(c + 1) * P], Mn[:, c, f * P:(f + 1) * P], ident[:, :])
                t = nc.tensor.transpose(bank[6][0:1, c * P:(c + 1) * P], nrm[:, 2, c:c + 1], ident[:, :])
            t.then_inc(s_mid, 1)
            waitmic(1, 1)
            for c in range(NP2):
                o = bank[7][:, c * P:(c + 1) * P]
                cs = slice(c * P, (c + 1) * P)
                mm(o, Wfx[:, 0, cs], MnT[:, 0, cs], True, False)
                mm(o, Wfx[:, 1, cs], MnT[:, 1, cs], False, False)
                m = mm(o, bfx[:, cs], nbT[:, cs], False, True)
            m.then_inc(s_mid, 1)
            waitmic()
            for c in range(NP2):
                mm(bank[4][:, c * P:(c + 1) * P], W3[:, 0, :], tokd[:, c, :])
                mm(bank[5][:, c * G:(c + 1) * G], W3[:, 1, :], tokc[:, c, :])
                m = mm(bank[6][:, c * P:(c + 1) * P], tokd[:, c, :], W3[:, 2, :])
            m.then_inc(s_mid, 1)
            waitmic(1, 1)
            for c in range(NP2):
                m = mm(bank[7][:, c * G:(c + 1) * G], qd[:, c, :], kc[:, c, :])
            m.then_inc(s_mid, 1)
            waitmic(2)
            for c in range(NP2):
                t = nc.tensor.transpose(bank[4][:, c * P:(c + 1) * P], ad[:, c, :], ident[:, :])
            t.then_inc(s_mid, 1)
            waitmic()
            for c in range(NP2):
                m = mm(bank[5][:, c * P:(c + 1) * P], vd[:, c, :], aT[:, c, :])
            m.then_inc(s_mid, 1)
            waitmic()
            for c in range(NP2):
                m = mm(bank[6 + c // 2][:, (c % 2) * F:(c % 2 + 1) * F], oT[:, c, :], Wo[:, c, :])
            m.then_inc(s_mid, 1)
            waitmic(1, 1)

            def product(b, k, first):
                pe.wait_ge(s_wl, b + 1)
                if not first:
                    pe.wait_ge(s_os, b - 1)
                for c in range(NP2):
                    m = mm(bank[4 + k][:, 0:F], stg[:, k, c * P:(c + 1) * P], Pm[:, c, :], c == 0, c == NP2 - 1)
                m.then_inc(s_o, 1)

            product(0, 0, True)
            product(1, 1, True)
            with pe.Fori(1, NB // 2) as i:
                for k in range(2):
                    product(i * 2 + k, k, False)
            product(LAST, 0, False)


_INS = ['x', 'src', 'dst', 'edge_weight', 'L0_gnn_W', 'L0_gnn_a1', 'L0_gnn_a2', 'L0_ffn_W_fx', 'L0_ffn_b_fx',
        'L0_ffn_W_x', 'L0_ffn_b_x', 'L0_ffn_W_slice', 'L0_ffn_b_slice', 'L0_ffn_W_q', 'L0_ffn_W_k', 'L0_ffn_W_v',
        'L0_ffn_W_out', 'L0_ffn_b_out', 'L0_ffn_temperature']


def kernel(**inputs):
    import numpy as _np
    import concourse.bacc as _bacc
    from concourse import mybir as _mybir
    from concourse.bass_utils import run_bass_kernel_spmd as _run

    nc = _bacc.Bacc("TRN2", target_bir_lowering=False, num_devices=1)
    arrays, args = {}, []
    for name in _INS:
        a = _np.ascontiguousarray(inputs[name])
        arrays[f"in_{name}_dram"] = a
        args.append(nc.dram_tensor(f"in_{name}_dram", a.shape, _mybir.dt.from_np(a.dtype), kind="ExternalInput").ap())
    out = nc.dram_tensor("out_0_dram", (N, F), F32, kind="ExternalOutput").ap()
    gtab = nc.dram_tensor("gated_rows_dram", (NB * P, GW), F32, kind="Internal").ap()
    srt = nc.dram_tensor("sorted_edges_dram", (2 * LL, 1), F32, kind="Internal").ap()
    ovs = nc.dram_tensor("overflow_sums_dram", (P, NB, GW), F32, kind="Internal").ap()
    build(nc, *args, out, gtab, srt, ovs)
    r = _run(nc, [arrays], core_ids=[0])
    return r.results[0]["out_0_dram"]
```
